# Optimizing a Trainium2 kernel written in Bass

```python
import numpy as np
import jax
import jax.numpy as jnp

def _softmax(x, axis=-1):
    return jax.nn.softmax(x, axis=axis)

def _gelu(x):
    return jax.nn.gelu(x, approximate=True)

def _silu(x):
    return jax.nn.silu(x)

def _sigmoid(x):
    return jax.nn.sigmoid(x)

def _layernorm(x, axis=-1, eps=1e-05):
    m = jnp.mean(x, axis=axis, keepdims=True)
    v = jnp.var(x, axis=axis, keepdims=True)
    return (x - m) / jnp.sqrt(v + eps)

def _scatter_add(tgt, idx, src, axis=0):
    return tgt.at[idx].add(src)

def _segment_sum(src, seg, n):
    return jax.ops.segment_sum(src, seg, n)
kernel_name = 'mk_hybrid_d1_jaxref_r8_e79665'

def setup_inputs(seed: int=0):
    np.random.seed(seed)
    _w = jnp.asarray

    def _L0_attn_a_setup():
        import jax, jax.numpy as jnp
        import numpy as np
        DIM = 128
        N_HEADS = 16
        HEAD_DIM = DIM // N_HEADS
        FREQS = [31.0, 37.0, 41.0, 43.0, 47.0]
        TWO_PI = 2.0 * float(np.pi)
        key = jax.random.key(seed)
        ks = jax.random.split(key, 16)
        B, L = (2, 128)
        s = 0.02
        inp = {'x': jax.random.normal(ks[0], (B, L, DIM), dtype=jnp.float32), 'Wq': jax.random.normal(ks[1], (DIM, DIM), dtype=jnp.float32) * s, 'bq': jnp.zeros((DIM,), dtype=jnp.float32), 'Wk': jax.random.normal(ks[2], (DIM, DIM), dtype=jnp.float32) * s, 'bk': jnp.zeros((DIM,), dtype=jnp.float32), 'Wv': jax.random.normal(ks[3], (DIM, DIM), dtype=jnp.float32) * s, 'bv': jnp.zeros((DIM,), dtype=jnp.float32), 'Wo': jax.random.normal(ks[4], (DIM, DIM), dtype=jnp.float32) * s, 'bo': jnp.zeros((DIM,), dtype=jnp.float32), 'alpha': jax.random.normal(ks[5], (N_HEADS, len(FREQS)), dtype=jnp.float32) * 0.1, 'phi': jax.random.uniform(ks[6], (N_HEADS, len(FREQS)), dtype=jnp.float32) * TWO_PI, 'temperature': jnp.ones((1,), dtype=jnp.float32), 'gamma': jnp.ones((DIM,), dtype=jnp.float32), 'beta': jnp.zeros((DIM,), dtype=jnp.float32)}
        return inp
    _L0_attn_a_in = _L0_attn_a_setup()

    def _L0_attn_b_setup():
        import jax, jax.numpy as jnp
        import numpy as np
        import math
        HIDDEN = 128
        HEADS = 16
        HEAD_DIM = HIDDEN // HEADS
        MAX_POS = 256
        BATCH = 2
        SEQ = 256
        key = jax.random.key(seed)
        ks = jax.random.split(key, 8)
        s = 0.02
        return {'hidden_states': jax.random.normal(ks[0], (BATCH, SEQ, HIDDEN), jnp.float32), 'Wq': jax.random.normal(ks[1], (HIDDEN, HIDDEN), jnp.float32) * s, 'bq': jnp.zeros((HIDDEN,), jnp.float32), 'Wk': jax.random.normal(ks[2], (HIDDEN, HIDDEN), jnp.float32) * s, 'bk': jnp.zeros((HIDDEN,), jnp.float32), 'Wv': jax.random.normal(ks[3], (HIDDEN, HIDDEN), jnp.float32) * s, 'bv': jnp.zeros((HIDDEN,), jnp.float32), 'dist_emb': jax.random.normal(ks[4], (2 * MAX_POS - 1, HEAD_DIM), jnp.float32) * s}
    _L0_attn_b_in = _L0_attn_b_setup()

    def _L0_ffn_setup():
        import jax, jax.numpy as jnp
        import numpy as np
        B, T, D, H, E, TOPK = (2, 256, 128, 512, 8, 2)

        def sq_relu(x):
            return jnp.square(jax.nn.relu(x))
        key = jax.random.key(seed)
        ks = jax.random.split(key, 6)
        s = 0.02
        return {'x': jax.random.normal(ks[0], (B, T, D), dtype=jnp.float32), 'W_router': jax.random.normal(ks[1], (D, E), dtype=jnp.float32) * s, 'W_up': jax.random.normal(ks[2], (E, D, H), dtype=jnp.float32) * s, 'W_down': jax.random.normal(ks[3], (E, H, D), dtype=jnp.float32) * s, 'W_sh_up': jax.random.normal(ks[4], (D, H), dtype=jnp.float32) * s, 'W_sh_down': jax.random.normal(ks[5], (H, D), dtype=jnp.float32) * s}
    _L0_ffn_in = _L0_ffn_setup()
    _d = {'L0_attn_a_x': _L0_attn_a_in['x'], 'L0_attn_a_Wq': _L0_attn_a_in['Wq'], 'L0_attn_a_bq': _L0_attn_a_in['bq'], 'L0_attn_a_Wk': _L0_attn_a_in['Wk'], 'L0_attn_a_bk': _L0_attn_a_in['bk'], 'L0_attn_a_Wv': _L0_attn_a_in['Wv'], 'L0_attn_a_bv': _L0_attn_a_in['bv'], 'L0_attn_a_Wo': _L0_attn_a_in['Wo'], 'L0_attn_a_bo': _L0_attn_a_in['bo'], 'L0_attn_a_alpha': _L0_attn_a_in['alpha'], 'L0_attn_a_phi': _L0_attn_a_in['phi'], 'L0_attn_a_temperature': _L0_attn_a_in['temperature'], 'L0_attn_a_gamma': _L0_attn_a_in['gamma'], 'L0_attn_a_beta': _L0_attn_a_in['beta'], 'L0_attn_b_Wq': _L0_attn_b_in['Wq'], 'L0_attn_b_bq': _L0_attn_b_in['bq'], 'L0_attn_b_Wk': _L0_attn_b_in['Wk'], 'L0_attn_b_bk': _L0_attn_b_in['bk'], 'L0_attn_b_Wv': _L0_attn_b_in['Wv'], 'L0_attn_b_bv': _L0_attn_b_in['bv'], 'L0_attn_b_dist_emb': _L0_attn_b_in['dist_emb'], 'L0_ffn_W_router': _L0_ffn_in['W_router'], 'L0_ffn_W_up': _L0_ffn_in['W_up'], 'L0_ffn_W_down': _L0_ffn_in['W_down'], 'L0_ffn_W_sh_up': _L0_ffn_in['W_sh_up'], 'L0_ffn_W_sh_down': _L0_ffn_in['W_sh_down']}
    _x0 = _d['L0_attn_a_x']
    _d['L0_attn_a_x'] = jax.random.normal(jax.random.fold_in(jax.random.key(seed), 1), (8, 512, 128), dtype=_x0.dtype)
    del _x0
    return _d

def reference(L0_attn_a_x, L0_attn_a_Wq, L0_attn_a_bq, L0_attn_a_Wk, L0_attn_a_bk, L0_attn_a_Wv, L0_attn_a_bv, L0_attn_a_Wo, L0_attn_a_bo, L0_attn_a_alpha, L0_attn_a_phi, L0_attn_a_temperature, L0_attn_a_gamma, L0_attn_a_beta, L0_attn_b_Wq, L0_attn_b_bq, L0_attn_b_Wk, L0_attn_b_bk, L0_attn_b_Wv, L0_attn_b_bv, L0_attn_b_dist_emb, L0_ffn_W_router, L0_ffn_W_up, L0_ffn_W_down, L0_ffn_W_sh_up, L0_ffn_W_sh_down):

    def _L0_attn_a_ref(x, Wq, bq, Wk, bk, Wv, bv, Wo, bo, alpha, phi, temperature, gamma, beta):
        import jax, jax.numpy as jnp
        import numpy as np
        DIM = 128
        N_HEADS = 16
        HEAD_DIM = DIM // N_HEADS
        FREQS = [31.0, 37.0, 41.0, 43.0, 47.0]
        TWO_PI = 2.0 * float(np.pi)
        B, L, D = x.shape
        H, hd = (N_HEADS, HEAD_DIM)
        q = (x @ Wq.T + bq).reshape(B, L, H, hd).transpose(0, 2, 1, 3)
        k = (x @ Wk.T + bk).reshape(B, L, H, hd).transpose(0, 2, 1, 3)
        v = (x @ Wv.T + bv).reshape(B, L, H, hd).transpose(0, 2, 1, 3)
        sim = jnp.einsum('bhid,bhjd->bhij', q, k) / jnp.sqrt(jnp.asarray(hd, x.dtype))
        temp = jnp.abs(temperature)[0] + 0.1
        sim = sim / temp
        scores = jnp.zeros_like(sim)
        for fi, freq in enumerate(FREQS):
            a = alpha[:, fi][None, :, None, None]
            p = phi[:, fi][None, :, None, None]
            scores = scores + a * jnp.sin(TWO_PI * sim / freq + p)
        w = jax.nn.sigmoid(scores)
        w = w / (jnp.sum(w, axis=-1, keepdims=True) + 1e-10)
        out = jnp.einsum('bhij,bhjd->bhid', w, v)
        out = out.transpose(0, 2, 1, 3).reshape(B, L, D)
        out = out @ Wo.T + bo
        mu = jnp.mean(out, axis=-1, keepdims=True)
        var = jnp.mean(jnp.square(out - mu), axis=-1, keepdims=True)
        return (out - mu) / jnp.sqrt(var + 1e-05) * gamma + beta

    def _L0_attn_b_ref(hidden_states, Wq, bq, Wk, bk, Wv, bv, dist_emb):
        import jax, jax.numpy as jnp
        import numpy as np
        import math
        HIDDEN = 128
        HEADS = 16
        HEAD_DIM = HIDDEN // HEADS
        MAX_POS = 256
        BATCH = 2
        SEQ = 256
        B, S, H = hidden_states.shape
        q = (hidden_states @ Wq.T + bq).reshape(B, S, HEADS, HEAD_DIM)
        k = (hidden_states @ Wk.T + bk).reshape(B, S, HEADS, HEAD_DIM)
        v = (hidden_states @ Wv.T + bv).reshape(B, S, HEADS, HEAD_DIM)
        scores = jnp.einsum('bqhd,bkhd->bhqk', q, k) / math.sqrt(HEAD_DIM)
        pos_q = jnp.arange(S)
        distance = pos_q[:, None] - pos_q[None, :]
        pos_emb = dist_emb[MAX_POS - 1 + distance]
        scores = scores + jnp.einsum('bqhd,qkd->bhqk', q, pos_emb)
        scores = scores + jnp.einsum('bkhd,qkd->bhqk', k, pos_emb)
        probs = jax.nn.softmax(scores, axis=-1)
        ctx = jnp.einsum('bhqk,bkhd->bqhd', probs, v)
        return ctx.reshape(B, S, H)

    def _L0_ffn_ref(x, W_router, W_up, W_down, W_sh_up, W_sh_down):
        import jax, jax.numpy as jnp
        import numpy as np
        B, T, D, H, E, TOPK = (2, 256, 128, 512, 8, 2)

        def sq_relu(x):
            return jnp.square(jax.nn.relu(x))
        Bb, Tt, Dd = x.shape
        x_flat = x.reshape(-1, Dd)
        N = x_flat.shape[0]
        logits = x_flat @ W_router
        probs = jax.nn.sigmoid(logits)
        topk_probs, topk_idx = jax.lax.top_k(probs, TOPK)
        topk_probs = topk_probs / (jnp.sum(topk_probs, axis=-1, keepdims=True) + 1e-06)
        combine = jnp.zeros((N, E), dtype=x.dtype).at[jnp.arange(N)[:, None], topk_idx].add(topk_probs)
        out = sq_relu(x_flat @ W_sh_up) @ W_sh_down
        for e in range(E):
            h = sq_relu(x_flat @ W_up[e])
            out = out + combine[:, e:e + 1] * (h @ W_down[e])
        return out.reshape(Bb, Tt, Dd)
    x = L0_attn_a_x
    x = x + _L0_attn_a_ref(_layernorm(x, axis=-1), L0_attn_a_Wq, L0_attn_a_bq, L0_attn_a_Wk, L0_attn_a_bk, L0_attn_a_Wv, L0_attn_a_bv, L0_attn_a_Wo, L0_attn_a_bo, L0_attn_a_alpha, L0_attn_a_phi, L0_attn_a_temperature, L0_attn_a_gamma, L0_attn_a_beta)
    x = x + _L0_ffn_ref(_layernorm(x, axis=-1), L0_ffn_W_router, L0_ffn_W_up, L0_ffn_W_down, L0_ffn_W_sh_up, L0_ffn_W_sh_down)
    x = x + _L0_attn_b_ref(_layernorm(x, axis=-1), L0_attn_b_Wq, L0_attn_b_bq, L0_attn_b_Wk, L0_attn_b_bk, L0_attn_b_Wv, L0_attn_b_bv, L0_attn_b_dist_emb)
    x = x + _L0_ffn_ref(_layernorm(x, axis=-1), L0_ffn_W_router, L0_ffn_W_up, L0_ffn_W_down, L0_ffn_W_sh_up, L0_ffn_W_sh_down)
    return x

_drawn_inputs = setup_inputs


def setup_inputs(seed=0):
    import zlib

    import numpy as np

    out = dict(_drawn_inputs(seed))
    spreads = {'L0_attn_a_bq': (0.0, 2.0),
     'L0_attn_a_bk': (0.0, 2.0),
     'L0_attn_a_bv': (0.0, 0.1),
     'L0_attn_a_bo': (0.0, 0.1),
     'L0_attn_a_gamma': (1.0, 0.2),
     'L0_attn_a_beta': (0.0, 0.1),
     'L0_attn_b_bq': (0.0, 2.0),
     'L0_attn_b_bk': (0.0, 2.0),
     'L0_attn_b_bv': (0.0, 0.1)}
    factors = {'L0_attn_a_Wq': 8.0,
     'L0_attn_a_Wk': 8.0,
     'L0_attn_a_Wv': 3.655,
     'L0_attn_a_alpha': 8.0,
     'L0_attn_a_phi': 8.0,
     'L0_attn_b_Wq': 8.0,
     'L0_attn_b_Wk': 8.0,
     'L0_attn_b_dist_emb': 8.0}
    for name, (base, spread) in spreads.items():
        noise = np.random.default_rng([zlib.crc32(name.encode()), seed]).standard_normal(out[name].shape)
        drawn = base * np.exp(spread * noise) if base else spread * noise
        out[name] = jnp.asarray(drawn.astype(out[name].dtype))
    for name, factor in factors.items():
        out[name] = (out[name] * factor).astype(out[name].dtype)
    return out
```

```python
from contextlib import ExitStack

import numpy as np

import concourse.bass as bass
from concourse import mybir

F32 = mybir.dt.float32
BF16 = mybir.dt.bfloat16
I32 = mybir.dt.int32
U32 = mybir.dt.uint32
ALU = mybir.AluOpType
ACT = mybir.ActivationFunctionType
AX = mybir.AxisListType

P = 128
B, L, D = 8, 512, 128
H, HD = 16, 8
QT = L // P
NT = B * QT
HG = 4
NG = B * H // HG
GPB = H // HG
VW = HD + 1
FREQS = (31.0, 37.0, 41.0, 43.0, 47.0)
NF = len(FREQS)
PE_F = 3
TWO_PI = 2.0 * float(np.pi)
E, HID = 8, 512
NE = E + 1
HT = HID // P
MAX_POS = 256
LEFT = "hhmhlm"
RIGHT = "hmhlhm"
NR = len(LEFT) * HD
ODD = 64
FRAC = 24
ROUND = float(3 * 2 ** 22)
WIN = 2 * L


def build(nc, a):
    ctx = ExitStack()
    with ctx:
        dram = {
            n: nc.dram_tensor(n, (B * H, NR, L), BF16, kind="Internal").ap()
            for n in ("qa_parts", "ka_parts", "qb_parts", "kb_parts", "ks_parts")
        }

        def sb(c, name, shape, dt=F32):
            return c.enter_context(nc.sbuf_tensor(name, shape, dt))

        def ps(c, name, shape, dt=F32):
            return c.enter_context(nc.psum_tensor(name, shape, dt))

        held = []

        def sem(c, name):
            held.append(nc.alloc_semaphore(name=name))
            return held[-1]

        def clear_semaphores():
            nc.clear_and_free_semaphores(held)
            nc.all_engine_barrier()
            held.clear()

        dram["wave_out"] = nc.dram_tensor("wave_out", (NG + 1, P, QT * HG * HD), F32, kind="Internal").ap()
        ident = sb(ctx, "ident", [P, P])
        V = sb(ctx, "V", [P, NG + 1, QT, HG, VW])
        mv = sb(ctx, "mv", [P, NT, 2])
        rstd = sb(ctx, "rstd", [P, NT])
        with ExitStack() as c:
            params = sb(c, "params", [P, NG, 2, HG * NF])
            big = sb(c, "big", [P, 2])
            with ExitStack() as c2:
                X = sb(c2, "X", [P, NT, D])
                first_block(nc, sem, a, X, ident, V)
                layer_norm(nc, sb, sem, "lna", X, mv, rstd)
                project_block(nc, sb, ps, sem, "a", a, X, V, ident, mv, rstd, dram, params, big)
            wave_attention(nc, sb, ps, sem, a, V, ident, dram, params)
        X = sb(ctx, "X2", [P, NT, D])
        wave_output(nc, sb, ps, sem, a, X, ident, mv, rstd, dram)
        layer_norm(nc, sb, sem, "lnf1", X, mv, rstd)
        experts(nc, sb, ps, sem, "f1", a, X, ident, mv, rstd)
        clear_semaphores()
        layer_norm(nc, sb, sem, "lnb", X, mv, rstd)
        project_block(nc, sb, ps, sem, "b", a, X, V, ident, mv, rstd, dram, None, None)
        distance_attention(nc, sb, ps, sem, a, X, V, ident, dram)
        layer_norm(nc, sb, sem, "lnf2", X, mv, rstd)
        experts(nc, sb, ps, sem, "f2", a, X, ident, mv, rstd)
        last_block(nc, sem, a, X)


def first_block(nc, sem, a, X, ident, V):
    with ExitStack() as c:
        loaded = sem(c, "x_loaded")
        cleared = sem(c, "ident_cleared")
        made = sem(c, "ident_made")
        block = c.enter_context(nc.Block())

        @block.sync
        def _(sp):
            sp.dma_start(X[:], a["x"].rearrange("b (t p) d -> p (b t) d", p=P)).then_inc(loaded, 16)
            sp.wait_ge(loaded, 16)

        @block.gpsimd
        def _(pool):
            pool.memset(ident[:], 0.0).then_inc(cleared, 1)
            pool.wait_ge(cleared, 1)
            pool.affine_select(out=ident[:], in_=ident[:], compare_op=ALU.not_equal, fill=1.0,
                               base=0, pattern=[[-1, P]], channel_multiplier=1).then_inc(made, 1)

        @block.vector
        def _(dve):
            dve.memset(V[:], 1.0).then_inc(made, 1)


def last_block(nc, sem, a, X):
    with ExitStack() as c:
        stored = sem(c, "out_stored")
        block = c.enter_context(nc.Block())

        @block.sync
        def _(sp):
            sp.dma_start(a["out"].rearrange("b (t p) d -> p (b t) d", p=P), X[:]).then_inc(stored, 16)
            sp.wait_ge(stored, 16)


def layer_norm(nc, sb, sem, name, src, mv, rstd):
    with ExitStack() as c:
        stats = sb(c, name + "_stats", [P, NT, 6])
        var = sb(c, name + "_var", [P, NT])
        root = sb(c, name + "_root", [P, NT])
        t1 = sb(c, name + "_t1", [P, NT])
        t2 = sb(c, name + "_t2", [P, NT])
        stat = sem(c, name + "_stat")
        aggr = sem(c, name + "_aggr")
        var_ready = sem(c, name + "_var_ready")
        root_ready = sem(c, name + "_root_ready")
        step = sem(c, name + "_step")
        block = c.enter_context(nc.Block())

        @block.vector
        def _(dve):
            for t in range(NT):
                dve.bn_stats(stats[:, t, :], src[:, t, :]).then_inc(stat, 1)
            for t in range(NT):
                dve.wait_ge(stat, t + 1)
                dve.bn_aggr(mv[:, t, :], stats[:, t, :]).then_inc(aggr, 1)
            dve.wait_ge(aggr, NT)
            dve.tensor_scalar(var[:], mv[:, :, 1], 1e-5, None, ALU.add).then_inc(var_ready, 1)
            dve.wait_ge(root_ready, 1)
            dve.reciprocal(t1[:], root[:]).then_inc(step, 1)
            dve.wait_ge(step, 1)
            dve.tensor_tensor(t2[:], t1[:], t1[:], ALU.mult).then_inc(step, 1)
            dve.wait_ge(step, 2)
            dve.scalar_tensor_tensor(out=t2[:], in0=t2[:], scalar=-0.5, in1=var[:],
                                     op0=ALU.mult, op1=ALU.mult).then_inc(step, 1)
            dve.wait_ge(step, 3)
            dve.tensor_scalar(t2[:], t2[:], 1.5, None, ALU.add).then_inc(step, 1)
            dve.wait_ge(step, 4)
            dve.tensor_tensor(rstd[:], t1[:], t2[:], ALU.mult).then_inc(step, 1)

        @block.scalar
        def _(act):
            act.wait_ge(var_ready, 1)
            act.activation(root[:], var[:], ACT.Sqrt).then_inc(root_ready, 1)


def project_block(nc, sb, ps, sem, layer, a, X, V, ident, mv, rstd, dram, params, big):
    wave = layer == "a"
    sides = [("q", "qa_parts", LEFT), ("k", "ka_parts", RIGHT)] if wave else \
            [("q", "qb_parts", LEFT), ("k", "kb_parts", LEFT), ("ks", "ks_parts", RIGHT)]
    NS = len(sides)
    with ExitStack() as c:
        wq = sb(c, layer + "_wq", [P, D])
        wk = sb(c, layer + "_wk", [P, D])
        wv = sb(c, layer + "_wv", [P, D])
        bq = sb(c, layer + "_bq", [P, 1])
        bk = sb(c, layer + "_bk", [P, 1])
        bv = sb(c, layer + "_bv", [P, D])
        qbias = sb(c, layer + "_qbias", [P, 1])
        qscale = sb(c, layer + "_qscale", [P, 1])
        xn = sb(c, layer + "_xn", [P, QT, D])
        xnT = sb(c, layer + "_xnT", [P, L])
        full = [sb(c, f"{layer}_full{s}", [P, L]) for s in range(NS)]
        rest = [sb(c, f"{layer}_rest{s}", [P, L]) for s in range(NS)]
        part = {(s, w): sb(c, f"{layer}_part{s}{w}", [P, L], BF16) for s in range(NS) for w in "hml"}
        top = sb(c, layer + "_top", [P, 2, B])
        topr = sb(c, layer + "_topr", [P, 2])
        topa = sb(c, layer + "_topa", [P, 2])
        raw = sb(c, layer + "_raw", [P, 2, H * NF])
        turns = sb(c, layer + "_turns", [P, H * NF])
        temp = sb(c, layer + "_temp", [P, 4])
        psT = ps(c, layer + "_psT", [P, L])
        psQ = ps(c, layer + "_psQ", [P, L])
        psK = ps(c, layer + "_psK", [P, L])
        psV = ps(c, layer + "_psV", [P, QT, D])
        small = sem(c, layer + "_weights_loaded")
        prep = sem(c, layer + "_prep")
        xn_ready = sem(c, layer + "_xn_ready")
        xT_ps = sem(c, layer + "_xT_ps")
        xT = sem(c, layer + "_xT")
        v_ps = sem(c, layer + "_v_ps")
        q_ps = sem(c, layer + "_q_ps")
        k_ps = sem(c, layer + "_k_ps")
        qk_taken = sem(c, layer + "_qk_taken")
        v_taken = sem(c, layer + "_v_taken")
        high = sem(c, layer + "_high")
        mid = sem(c, layer + "_mid")
        residue = sem(c, layer + "_residue")
        low = sem(c, layer + "_low")
        stored = [sem(c, f"{layer}_stored{s}") for s in range(NS)]
        topped = sem(c, layer + "_topped")
        block = c.enter_context(nc.Block())
        nload = 6 + (3 if wave else 0)

        @block.sync
        def _(sp):
            for t, src in ((wq, "wq"), (wk, "wk"), (wv, "wv")):
                sp.dma_start(t[:], a[layer + "_" + src]).then_inc(small, 16)
            for t, src in ((bq, "bq"), (bk, "bk")):
                sp.dma_start(t[:], a[layer + "_" + src]).then_inc(small, 16)
            sp.dma_start(bv[:], a[layer + "_bv"].to_broadcast((P, D))).then_inc(small, 16)
            if wave:
                sp.dma_start(temp[:, 0:1], a["temperature"].to_broadcast((P, 1))).then_inc(small, 16)
                sp.dma_start(raw[:, 0, :], a["phi"].to_broadcast((P, H * NF))).then_inc(small, 16)
                sp.dma_start(raw[:, 1, :], a["alpha"].to_broadcast((P, H * NF))).then_inc(small, 16)
            with sp.Fori(0, B) as b:
                for s, (_, dst, order) in enumerate(sides):
                    for r, w in enumerate(order):
                        if r == 0:
                            sp.wait_ge(high, b * NS + s + 1)
                        if w == "l":
                            sp.wait_ge(low, b * NS + s + 1)
                        if w == "m":
                            sp.wait_ge(mid, b * NS + s + 1)
                        sp.dma_start(
                            dram[dst][bass.ds(b * H, H), r * HD:(r + 1) * HD, :],
                            part[s, w][:]).then_inc(stored[s], 16)
            for s in range(NS):
                sp.wait_ge(stored[s], 16 * len(LEFT) * (B + 1))

        @block.vector
        def _(dve):
            dve.wait_ge(small, 16 * nload)
            if wave:
                dve.tensor_scalar(temp[:, 1:2], temp[:, 0:1], -1.0, None, ALU.mult).then_inc(prep, 1)
                dve.wait_ge(prep, 1)
                dve.tensor_tensor(temp[:, 2:3], temp[:, 0:1], temp[:, 1:2], ALU.max).then_inc(prep, 1)
                dve.wait_ge(prep, 2)
                dve.tensor_scalar(temp[:, 3:4], temp[:, 2:3], 0.1, float(np.sqrt(HD)), ALU.add,
                                  ALU.mult).then_inc(prep, 1)
                dve.wait_ge(prep, 3)
                dve.reciprocal(qscale[:], temp[:, 3:4]).then_inc(prep, 1)
                dve.wait_ge(prep, 4)
                dve.tensor_tensor(qbias[:], bq[:], qscale[:], ALU.mult).then_inc(prep, 1)
                dve.tensor_scalar(raw[:, 0, :], raw[:, 0, :], 1.0 / TWO_PI, None, ALU.mult).then_inc(prep, 1)
                dve.wait_ge(prep, 6)
                dve.tensor_scalar(turns[:], raw[:, 0, :], ROUND, ROUND, ALU.add, ALU.subtract).then_inc(prep, 1)
                dve.wait_ge(prep, 7)
                dve.tensor_tensor(raw[:, 0, :], raw[:, 0, :], turns[:], ALU.subtract).then_inc(prep, 1)
                dve.wait_ge(prep, 8)
                dve.tensor_scalar(raw[:, 0, :], raw[:, 0, :], float(2 ** FRAC), None, ALU.mult).then_inc(prep, 1)
                dve.wait_ge(prep, 9)
                for b in range(B):
                    for w in range(2):
                        dve.tensor_copy(params[:, b * GPB:(b + 1) * GPB, w, :],
                                        raw[:, w, :].rearrange("p (g n) -> p g n", g=GPB)).then_inc(prep, 1)
            else:
                dve.memset(qscale[:], 1.0).then_inc(prep, 1)
                dve.tensor_copy(qbias[:], bq[:]).then_inc(prep, 1)
            with dve.Fori(0, B) as b:
                for t in range(QT):
                    if t == 0:
                        dve.wait_ge(xT_ps, b + 1)
                    dve.tensor_scalar(xn[:, t, :], X[:, bass.ds(b * QT + t, 1), :],
                                      mv[:, bass.ds(b * QT + t, 1), 0], rstd[:, bass.ds(b * QT + t, 1)],
                                      ALU.subtract, ALU.mult).then_inc(xn_ready, 1)
                dve.wait_ge(v_ps, b + 1)
                for t in range(QT):
                    dve.tensor_tensor(
                        V[:, bass.ds(b * GPB + 1, GPB), t, :, 0:HD],
                        psV[:, t, :].rearrange("p (g h d) -> p g h d", g=GPB, h=HG),
                        bv[:].rearrange("p (g h d) -> p g h d", g=GPB, h=HG), ALU.add).then_inc(v_taken, 1)
                for s in range(NS):
                    dve.wait_ge(high, b * NS + s + 1)
                    if wave:
                        dve.tensor_reduce(top[:, s, bass.ds(b, 1)], full[s][:], AX.X, ALU.max,
                                          apply_absolute_value=True).then_inc(topped, 1)
                    dve.tensor_tensor(rest[s][:], full[s][:], part[s, "h"][:], ALU.subtract).then_inc(residue, 1)
                for s in range(NS):
                    dve.wait_ge(mid, b * NS + s + 1)
                    dve.wait_ge(stored[s], b * (16 * len(LEFT)) + 16 * len(LEFT))
                    dve.tensor_tensor(part[s, "l"][:], rest[s][:], part[s, "m"][:], ALU.subtract).then_inc(low, 1)
            if wave:
                dve.wait_ge(topped, NS * B)
                dve.tensor_reduce(topr[:], top[:], AX.X, ALU.max).then_inc(topped, 1)

        if wave:
            @block.gpsimd
            def _(pool):
                pool.wait_ge(topped, NS * B + 1)
                pool.partition_all_reduce(topa[:], topr[:], P, bass.bass_isa.ReduceOp.max).then_inc(topped, 1)
                pool.wait_ge(topped, NS * B + 2)
                pool.tensor_tensor(big[:, 0:1], topa[:, 0:1], topa[:, 1:2], ALU.mult).then_inc(topped, 1)

        @block.scalar
        def _(act):
            act.wait_ge(prep, 9 + 2 * B if wave else 2)
            with act.Fori(0, B) as b:
                act.wait_ge(xT_ps, b + 2)
                act.copy(xnT[:], psT[:]).then_inc(xT, 1)
                for s, (side, _, _) in enumerate(sides):
                    act.wait_ge(stored[s], b * (16 * len(LEFT)) + 16 * len(LEFT))
                    if side == "q":
                        act.wait_ge(q_ps, b + 1)
                        act.wait_ge(residue, b * NS + NS)
                        act.activation(full[s][:], psQ[:], ACT.Identity, bias=qbias[:], scale=qscale[:]).then_inc(qk_taken, 1)
                    elif side == "k":
                        act.wait_ge(k_ps, b + 1)
                        act.activation(full[s][:], psK[:], ACT.Identity, bias=bk[:]).then_inc(qk_taken, 1)
                    else:
                        act.wait_ge(qk_taken, b * NS + NS + 2)
                        act.mul(full[s][:], full[s - 1][:], float(1.0 / np.sqrt(HD))).then_inc(qk_taken, 1)
                    act.wait_ge(qk_taken, b * NS + s + 1 + NS)
                    act.copy(part[s, "h"][:], full[s][:]).then_inc(high, 1)
                for s in range(NS):
                    act.wait_ge(residue, b * NS + s + 1 + NS)
                    act.copy(part[s, "m"][:], rest[s][:]).then_inc(mid, 1)

        @block.tensor
        def _(pe):
            pe.sem_inc(xT_ps, 1)
            pe.sem_inc(qk_taken, NS)
            pe.sem_inc(residue, NS)
            pe.sem_inc(v_taken, QT)
            for s in range(NS):
                pe.sem_inc(stored[s], 16 * len(LEFT))
            pe.wait_ge(small, 16 * nload)
            with pe.Fori(0, B) as b:
                for t in range(QT):
                    pe.wait_ge(xn_ready, b * QT + t + 1)
                    mm = pe.transpose(psT[:, t * P:(t + 1) * P], xn[:, t, :], ident[:])
                mm.then_inc(xT_ps, 1)
                pe.wait_ge(xT, b + 1)
                pe.wait_ge(v_taken, b * QT + QT)
                for t in range(QT):
                    mm = pe.matmul(psV[:, t, :], xnT[:, t * P:(t + 1) * P], wv[:], start=True, stop=True)
                mm.then_inc(v_ps, 1)
                pe.wait_ge(qk_taken, b * NS + NS)
                pe.matmul(psQ[:], wq[:], xnT[:], start=True, stop=True).then_inc(q_ps, 1)
                pe.matmul(psK[:], wk[:], xnT[:], start=True, stop=True).then_inc(k_ps, 1)


def wave_attention(nc, sb, ps, sem, a, V, ident, dram, params):
    N = QT * L
    HALF = N // 2
    SR, XR, AR = 2, 4, 2 * HG
    DV_F = NF - PE_F
    ADDS = 2 * DV_F
    C_SPS, C_SREADY, C_TURNED, C_SINE, C_USED = 2 * 2 * HG, 2, 2 * HG * NF, NF, 2 * PE_F
    C_ADDED, C_DIAG, C_OUT, C_TAKEN, C_STORED = 2 * HG * ADDS, 2 * HG, 1, 1, 16
    with ExitStack() as c:
        qp = sb(c, "qp", [NR, 2, HG, L], BF16)
        kp = sb(c, "kp", [NR, 2, HG, L], BF16)
        s = sb(c, "s", [P, SR, N])
        angle = sb(c, "angle", [P, XR, N], I32)
        wave = sb(c, "wave", [P, NF, N])
        score = sb(c, "score", [P, AR, N])
        par = sb(c, "par", [P, 2, 2, HG * NF])
        diag = sb(c, "diag", [P, 2, PE_F, P])
        rec = sb(c, "rec", [P, HG, QT])
        og = sb(c, "og", [P, 2, QT, HG, HD])
        psS = ps(c, "psS", [P, 2, L])
        psA = ps(c, "psA", [P, QT, L])
        psO = ps(c, "psO", [P, HG, QT, VW])
        qk_loaded = [sem(c, f"qk_loaded{i}") for i in range(2)]
        s_ps = sem(c, "s_ps")
        s_ready = sem(c, "s_ready")
        turned = sem(c, "turned")
        cut = sem(c, "cut")
        sine = sem(c, "sine")
        used = sem(c, "sine_used")
        par_ready = sem(c, "par_ready")
        diag_ready = sem(c, "diag_ready")
        added = sem(c, "added")
        weighed = sem(c, "weighed")
        out_ps = sem(c, "out_ps")
        rec_ready = sem(c, "rec_ready")
        out_taken = sem(c, "out_taken")
        out_stored = [sem(c, f"out_stored{i}") for i in range(2)]
        cleared = sem(c, "cleared")
        block = c.enter_context(nc.Block())

        def load(sp, g, u):
            for dst, src in ((qp, "qa_parts"), (kp, "ka_parts")):
                sp.dma_start(dst[:, u, :, :], dram[src][bass.ds(g * HG, HG), :, :]
                             .rearrange("h r n -> r h n")).then_inc(qk_loaded[u], 16)

        @block.sync
        def _(sp):
            for u in range(2):
                load(sp, u, u)

            def pair(gg, last):
                for u in range(2):
                    g = gg * 2 + u
                    sp.wait_ge(out_taken, g + 1 + C_TAKEN)
                    sp.dma_start(dram["wave_out"][bass.ds(g, 1), :, :].rearrange("g p n -> p (g n)"),
                                 og[:, u, :, :, :].rearrange("p q h d -> p (q h d)")).then_inc(out_stored[u], 16)
                    if not last:
                        sp.wait_ge(s_ps, (g + 1) * 2 * HG + C_SPS)
                        load(sp, g + 2, u)

            with sp.Fori(0, NG // 2 - 1) as gg:
                pair(gg, False)
            pair(NG // 2 - 1, True)
            sp.wait_ge(out_taken, NG + 1 + C_TAKEN)
            sp.dma_start(dram["wave_out"][NG, :, :], og[:, 0, :, :, :].rearrange("p q h d -> p (q h d)"))\
              .then_inc(out_stored[0], 16)
            sp.wait_ge(out_stored[0], 16 * (NG // 2 + 1) + C_STORED)
            sp.wait_ge(out_stored[1], 16 * (NG // 2) + C_STORED)

        @block.gpsimd
        def _(pool):
            with pool.Fori(0, NG // 2) as gg:
                for u in range(2):
                    g = gg * 2 + u
                    pool.wait_ge(added, g * HG * ADDS + C_ADDED - HG * ADDS)
                    pool.wait_ge(turned, g * HG * NF + C_TURNED - HG * NF)
                    pool.wait_ge(diag_ready, g * HG + C_DIAG - HG)
                    pool.tensor_copy(par[:, u, :, :], params[:, bass.ds(g, 1), :, :]
                                     .rearrange("p a w n -> p (a w) n")).then_inc(par_ready, 1)
                    pool.wait_ge(par_ready, g + 1)
                    for h in range(HG):
                        pool.wait_ge(used, (g * HG + h) * PE_F - PE_F + C_USED)
                        for f in range(PE_F):
                            ins = pool.tensor_tensor(diag[:, h % 2, f, :], ident[:],
                                                     par[:, u, 1, h * NF + f:h * NF + f + 1]
                                                     .to_broadcast((P, P)), ALU.mult)
                        ins.then_inc(diag_ready, 1)

        @block.tensor
        def _(pe):
            for credit, n in ((s_ps, C_SPS), (s_ready, C_SREADY), (turned, C_TURNED), (sine, C_SINE),
                              (used, C_USED), (added, C_ADDED), (diag_ready, C_DIAG),
                              (out_ps, C_OUT), (out_taken, C_TAKEN),
                              (out_stored[0], C_STORED), (out_stored[1], C_STORED)):
                pe.sem_inc(credit, n)

            def make_scores(n, u, h, half):
                pe.wait_ge(s_ready, n * 2 + half + C_SREADY)
                for k in range(2):
                    kt = half * 2 + k
                    mm = pe.matmul(psS[:, k, :], kp[:, u, h, kt * P:(kt + 1) * P], qp[:, u, h, :],
                                   start=True, stop=True)
                mm.then_inc(s_ps, 1)

            def values(g, slot):
                for h in range(HG):
                    pe.wait_ge(weighed, g * HG + h + 1)
                    if h == 0:
                        pe.wait_ge(out_taken, g + C_TAKEN)
                    for qt in range(QT):
                        for kt in range(QT):
                            mm = pe.matmul(psO[:, h, qt, :],
                                           score[:, slot * HG + h, kt * L + qt * P:kt * L + (qt + 1) * P],
                                           V[:, bass.ds(g, 1), kt, h, :].rearrange("p a d -> p (a d)"),
                                           start=(kt == 0), stop=(kt == QT - 1))
                mm.then_inc(out_ps, 1)

            def pair(gg, last):
                for u in range(2):
                    g = gg * 2 + u
                    for h in range(HG):
                        n = g * HG + h
                        final = last and u == 1 and h == HG - 1
                        nu, nh = (u, h + 1) if h < HG - 1 else (1 - u, 0)
                        if h == HG - 1 and not final:
                            pe.wait_ge(qk_loaded[nu], (gg + 1 + u) * 32)
                        if not final:
                            make_scores(n + 1, nu, nh, 0)
                        pe.wait_ge(diag_ready, n + 1 + C_DIAG)
                        for f in range(PE_F):
                            pe.wait_ge(sine, n * NF + f + 1 + C_SINE)
                            for kt in range(QT):
                                if f == 0 and kt % 2 == 0:
                                    pe.wait_ge(added, n * ADDS - ADDS + kt // 2 + 1 + C_ADDED)
                                mm = pe.matmul(psA[:, kt, :], diag[:, h % 2, f, :],
                                               wave[:, f, kt * L:(kt + 1) * L],
                                               start=(f == 0), stop=(f == PE_F - 1), skip_group_check=True)
                            mm.then_inc(used, 1)
                            if f == 0 and not final:
                                make_scores(n + 1, nu, nh, 1)
                        if h == 1:
                            values(g, 1 - u)

            pe.wait_ge(qk_loaded[0], 32)
            make_scores(0, 0, 0, 0)
            make_scores(0, 0, 0, 1)
            with pe.Fori(0, NG // 2 - 1) as gg:
                pair(gg, False)
            pair(NG // 2 - 1, True)
            values(NG, 1)

        @block.scalar
        def _(act):
            def take_scores(n, h, half):
                act.wait_ge(s_ps, n * 2 + half + 1 + C_SPS)
                act.wait_ge(turned, n * NF - NF + C_TURNED)
                act.copy(s[:, h % SR, half * HALF:(half + 1) * HALF],
                         psS[:].rearrange("p a n -> p (a n)")).then_inc(s_ready, 1)

            def sigmoids(g, slot):
                for h in range(HG):
                    act.wait_ge(added, g * HG * ADDS - (HG - 1 - h) * ADDS + C_ADDED)
                    act.activation(score[:, slot * HG + h, :], score[:, slot * HG + h, :], ACT.Sigmoid)\
                       .then_inc(weighed, 1)

            def pair(gg, last):
                for u in range(2):
                    g = gg * 2 + u
                    for h in range(HG):
                        n = g * HG + h
                        final = last and u == 1 and h == HG - 1
                        if not final:
                            take_scores(n + 1, h + 1, 0)
                        for f in range(NF):
                            if f == 1 and not final:
                                take_scores(n + 1, h + 1, 1)
                            act.wait_ge(cut, n * NF + f + 1)
                            if f < PE_F:
                                act.wait_ge(used, n * PE_F - PE_F + f + 1 + C_USED)
                            else:
                                act.wait_ge(added, n * ADDS - ADDS + 2 * (f - PE_F + 1) + C_ADDED)
                            act.activation(wave[:, f, :], angle[:, ((u * HG + h) * NF + f) % XR, :], ACT.Sin,
                                           scale=float(TWO_PI / 2.0 ** 32)).then_inc(sine, 1)
                        if h == 0:
                            sigmoids(g, 1 - u)

            take_scores(0, 0, 0)
            take_scores(0, 0, 1)
            act.wait_ge(cleared, 1)
            with act.Fori(0, NG // 2 - 1) as gg:
                pair(gg, False)
            pair(NG // 2 - 1, True)
            sigmoids(NG, 1)

        @block.vector
        def _(dve):
            def make_angle(i, g, u, h, f):
                x = ((u * HG + h) * NF + f) % XR
                if f == 0:
                    dve.wait_ge(s_ready, g * 2 * HG + (h + 1) * 2 + C_SREADY)
                dve.wait_ge(sine, i + 1 - XR + C_SINE)
                dve.tensor_scalar(angle[:, x, :], s[:, h % SR, :], float(2 ** FRAC) / FREQS[f],
                                  par[:, u, 0, h * NF + f:h * NF + f + 1],
                                  ALU.mult, ALU.add).then_inc(turned, 1)
                dve.wait_ge(turned, i + 1 + C_TURNED)
                dve.tensor_scalar(angle[:, x, :], angle[:, x, :], 32 - FRAC, None,
                                  ALU.logical_shift_left).then_inc(cut, 1)

            def add_sine(n, u, h, f):
                dve.wait_ge(sine, n * NF + f + 1 + C_SINE)
                for half in range(2):
                    cols = slice(half * HALF, (half + 1) * HALF)
                    if f == PE_F:
                        dve.wait_ge(used, n * PE_F + PE_F + C_USED)
                        other = psA[:, half * 2:half * 2 + 2, :].rearrange("p a n -> p (a n)")
                    else:
                        dve.wait_ge(added, n * ADDS + (f - PE_F - 1) * 2 + half + 1 + C_ADDED)
                        other = score[:, u * HG + h, cols]
                    dve.scalar_tensor_tensor(
                        out=score[:, u * HG + h, cols], in0=wave[:, f, cols],
                        scalar=par[:, u, 1, h * NF + f:h * NF + f + 1], in1=other,
                        op0=ALU.mult, op1=ALU.add).then_inc(added, 1)

            def outputs(g, gg, slot):
                dve.wait_ge(out_ps, g + 1 + C_OUT)
                dve.tensor_scalar(rec[:], psO[:, :, :, HD], 1e-10, None, ALU.add).then_inc(rec_ready, 1)
                dve.wait_ge(rec_ready, g * 2 + 1)
                dve.reciprocal(rec[:], rec[:]).then_inc(rec_ready, 1)
                dve.wait_ge(rec_ready, g * 2 + 2)
                dve.wait_ge(out_stored[slot], gg * 16 + C_STORED)
                dve.tensor_tensor(og[:, slot, :, :, :].rearrange("p q h d -> p h q d"), psO[:, :, :, 0:HD],
                                  rec[:].rearrange("p h (q o) -> p h q o", o=1).to_broadcast((P, HG, QT, HD)),
                                  ALU.mult).then_inc(out_taken, 1)

            def pair(gg, last):
                for u in range(2):
                    g = gg * 2 + u
                    for h in range(HG):
                        n = g * HG + h
                        final = last and u == 1 and h == HG - 1
                        if h == 0:
                            dve.wait_ge(out_ps, g + C_OUT)
                        nu, nh, ng = (u, h + 1, g) if h < HG - 1 else (1 - u, 0, g + 1)
                        make_angle(n * NF + 4, g, u, h, 4)
                        if h == HG - 1 and not final:
                            dve.wait_ge(par_ready, g + 2)
                        if not final:
                            for f in range(3):
                                make_angle(n * NF + NF + f, ng, nu, nh, f)
                        add_sine(n, u, h, PE_F)
                        if not final:
                            make_angle(n * NF + NF + 3, ng, nu, nh, 3)
                        for f in range(PE_F + 1, NF):
                            add_sine(n, u, h, f)
                        if h == 1:
                            outputs(g, gg, u)

            dve.memset(score[:, HG:2 * HG, :], 0.0).then_inc(cleared, 1)
            dve.wait_ge(par_ready, 1)
            for f in range(4):
                make_angle(f, 0, 0, 0, f)
            with dve.Fori(0, NG // 2 - 1) as gg:
                pair(gg, False)
            pair(NG // 2 - 1, True)
            outputs(NG, NG // 2, 0)


def wave_output(nc, sb, ps, sem, a, X, ident, mv, rstd, dram):
    with ExitStack() as c:
        Y = sb(c, "Y", [P, NT, D])
        with ExitStack() as c2:
            wo = sb(c2, "wo", [P, D])
            bo = sb(c2, "bo", [P, D])
            o = sb(c2, "o", [P, 2, GPB, QT, HG * HD])
            oq = sb(c2, "oq", [P, QT, D])
            oT = sb(c2, "oT", [P, L])
            psT = ps(c2, "psOT", [P, L])
            psY = ps(c2, "psY", [P, QT, D])
            loaded = sem(c2, "wo_loaded")
            o_loaded = [sem(c2, f"o_loaded{i}") for i in range(2)]
            o_ready = sem(c2, "o_ready")
            t_ps = sem(c2, "oT_ps")
            t_ready = sem(c2, "oT_ready")
            y_ps = sem(c2, "y_ps")
            y_ready = sem(c2, "y_ready")
            block = c2.enter_context(nc.Block())

            @block.sync
            def _(sp):
                sp.sem_inc(t_ps, 1)
                sp.sem_inc(y_ready, QT)
                sp.sem_inc(o_ready, 2)
                sp.dma_start(wo[:], a["wo"]).then_inc(loaded, 16)
                sp.dma_start(bo[:], a["bo"].to_broadcast((P, D))).then_inc(loaded, 16)
                sp.dma_start(X[:], a["x"].rearrange("b (t p) d -> p (b t) d", p=P)).then_inc(loaded, 16)
                with sp.Fori(0, B // 2) as bb:
                    for u in range(2):
                        sp.wait_ge(o_ready, bb * 2 + u + 1)
                        sp.dma_start(o[:, u, :, :, :].rearrange("p g q n -> p g (q n)"),
                                     dram["wave_out"][bass.ds((bb * 2 + u) * GPB + 1, GPB), :, :]
                                     .rearrange("g p n -> p g n")).then_inc(o_loaded[u], 16)
                sp.wait_ge(loaded, 48)

            @block.scalar
            def _(act):
                with act.Fori(0, B // 2) as bb:
                    for u in range(2):
                        b = bb * 2 + u
                        act.wait_ge(t_ps, b + 1)
                        act.wait_ge(o_loaded[u], bb * 16 + 16)
                        act.copy(oq[:].rearrange("p q (g n) -> p g q n", g=GPB), o[:, u, :, :, :])\
                           .then_inc(o_ready, 1)
                        act.wait_ge(t_ps, b + 2)
                        act.copy(oT[:], psT[:]).then_inc(t_ready, 1)

            @block.tensor
            def _(pe):
                pe.wait_ge(loaded, 48)
                with pe.Fori(0, B) as b:
                    pe.wait_ge(o_ready, b + 3)
                    for qt in range(QT):
                        mm = pe.transpose(psT[:, qt * P:(qt + 1) * P], oq[:, qt, :], ident[:])
                    mm.then_inc(t_ps, 1)
                    pe.wait_ge(t_ready, b + 1)
                    pe.wait_ge(y_ready, b * QT + QT)
                    for qt in range(QT):
                        mm = pe.matmul(psY[:, qt, :], oT[:, qt * P:(qt + 1) * P], wo[:], start=True, stop=True)
                    mm.then_inc(y_ps, 1)

            @block.vector
            def _(dve):
                dve.wait_ge(loaded, 48)
                with dve.Fori(0, B) as b:
                    dve.wait_ge(y_ps, b + 1)
                    for qt in range(QT):
                        dve.tensor_tensor(Y[:, bass.ds(b * QT + qt, 1), :].rearrange("p a n -> p (a n)"),
                                          psY[:, qt, :], bo[:], ALU.add).then_inc(y_ready, 1)
        layer_norm(nc, sb, sem, "lny", Y, mv, rstd)
        with ExitStack() as c2:
            gamma = sb(c2, "gamma", [P, D])
            beta = sb(c2, "beta", [P, D])
            loaded = sem(c2, "gamma_loaded")
            step = sem(c2, "apply")
            block = c2.enter_context(nc.Block())
            HALF_T = NT // 2

            @block.sync
            def _(sp):
                sp.dma_start(gamma[:], a["gamma"].to_broadcast((P, D))).then_inc(loaded, 16)
                sp.dma_start(beta[:], a["beta"].to_broadcast((P, D))).then_inc(loaded, 16)
                sp.wait_ge(loaded, 32)

            @block.vector
            def _(dve):
                for t in range(NT):
                    dve.tensor_scalar(Y[:, t, :], Y[:, t, :], mv[:, t, 0:1], rstd[:, t:t + 1],
                                      ALU.subtract, ALU.mult).then_inc(step, 1)
                dve.wait_ge(loaded, 32)
                dve.wait_ge(step, NT)
                wide = (P, NT, D)
                dve.tensor_tensor(Y[:], Y[:], gamma[:].rearrange("p (o d) -> p o d", o=1).to_broadcast(wide),
                                  ALU.mult).then_inc(step, 1)
                dve.tensor_tensor(X[:], X[:], beta[:].rearrange("p (o d) -> p o d", o=1).to_broadcast(wide),
                                  ALU.add).then_inc(step, 1)
                dve.wait_ge(step, NT + 2)
                dve.tensor_tensor(X[:], X[:], Y[:], ALU.add).then_inc(step, 1)


def experts(nc, sb, ps, sem, name, a, X, ident, mv, rstd):
    with ExitStack() as c:
        xnT = sb(c, name + "_xnT", [P, B, L])
        comb = sb(c, name + "_comb", [P, NT, NE])
        with ExitStack() as c2:
            route(nc, c2, sb, ps, sem, name, a, X, ident, mv, rstd, xnT, comb)
        with ExitStack() as c2:
            feed_forward(nc, c2, sb, ps, sem, name, a, X, xnT, comb)


def route(nc, c, sb, ps, sem, name, a, X, ident, mv, rstd, xnT, comb):
    wr = sb(c, name + "_wr", [P, E])
    xn = sb(c, name + "_xn", [P, 2, QT, D])
    prob = sb(c, name + "_prob", [P, NT, E])
    top = sb(c, name + "_top", [P, NT, E])
    index = sb(c, name + "_index", [P, NT, E], U32)
    indexf = sb(c, name + "_indexf", [P, NT, 2])
    iota = sb(c, name + "_iota", [P, E])
    first = sb(c, name + "_first", [P, NT, E])
    total = sb(c, name + "_total", [P, NT])
    psT = ps(c, name + "_psT", [P, 2, L])
    psR = ps(c, name + "_psR", [P, NT, E])
    loaded = sem(c, name + "_wr_loaded")
    xn_ready = sem(c, name + "_xn_ready")
    t_ps = sem(c, name + "_t_ps")
    t_ready = sem(c, name + "_t_ready")
    logits = sem(c, name + "_logits")
    prob_ready = sem(c, name + "_prob_ready")
    iota_ready = sem(c, name + "_iota_ready")
    step = sem(c, name + "_route_step")
    block = c.enter_context(nc.Block())

    @block.sync
    def _(sp):
        sp.dma_start(wr[:], a["w_router"]).then_inc(loaded, 16)
        sp.wait_ge(loaded, 16)

    @block.gpsimd
    def _(pool):
        pool.iota(iota[:], pattern=[[1, E]], base=0, channel_multiplier=0,
                  allow_small_or_imprecise_dtypes=True).then_inc(iota_ready, 1)

    @block.vector
    def _(dve):
        for t in range(NT):
            if t >= 2 * QT and t % QT == 0:
                dve.wait_ge(t_ps, t // QT - 1)
            dve.tensor_scalar(xn[:, (t // QT) % 2, t % QT, :], X[:, t, :], mv[:, t, 0:1], rstd[:, t:t + 1],
                              ALU.subtract, ALU.mult).then_inc(xn_ready, 1)
        dve.wait_ge(prob_ready, 1)
        for t in range(NT):
            dve.max(top[:, t, :], prob[:, t, :]).then_inc(step, 1)
        for t in range(NT):
            dve.wait_ge(step, t + 1)
            dve.max_index(index[:, t, :], top[:, t, :], prob[:, t, :]).then_inc(step, 1)
        dve.wait_ge(step, 2 * NT)
        dve.tensor_copy(indexf[:], index[:, :, 0:2]).then_inc(step, 1)
        dve.tensor_tensor(total[:], top[:, :, 0], top[:, :, 1], ALU.add).then_inc(step, 1)
        dve.wait_ge(step, 2 * NT + 2)
        dve.tensor_scalar(total[:], total[:], 1e-6, None, ALU.add).then_inc(step, 1)
        dve.wait_ge(step, 2 * NT + 3)
        dve.reciprocal(total[:], total[:]).then_inc(step, 1)
        dve.wait_ge(iota_ready, 1)
        wide = (P, NT, E)
        places = iota[:].rearrange("p (o e) -> p o e", o=1).to_broadcast(wide)
        dve.wait_ge(step, 2 * NT + 4)
        dve.tensor_tensor(first[:], places, indexf[:, :, 0:1].to_broadcast(wide), ALU.is_equal).then_inc(step, 1)
        dve.tensor_tensor(comb[:, :, 0:E], places, indexf[:, :, 1:2].to_broadcast(wide), ALU.is_equal)\
           .then_inc(step, 1)
        dve.memset(comb[:, :, E:NE], 1.0).then_inc(step, 1)
        dve.wait_ge(step, 2 * NT + 6)
        dve.tensor_tensor(first[:], first[:], top[:, :, 0:1].to_broadcast(wide), ALU.mult).then_inc(step, 1)
        dve.tensor_tensor(comb[:, :, 0:E], comb[:, :, 0:E], top[:, :, 1:2].to_broadcast(wide), ALU.mult)\
           .then_inc(step, 1)
        dve.wait_ge(step, 2 * NT + 9)
        dve.tensor_tensor(comb[:, :, 0:E], comb[:, :, 0:E], first[:], ALU.add).then_inc(step, 1)
        dve.wait_ge(step, 2 * NT + 10)
        dve.tensor_tensor(comb[:, :, 0:E], comb[:, :, 0:E],
                          total[:].rearrange("p (t o) -> p t o", o=1).to_broadcast(wide), ALU.mult)\
           .then_inc(step, 1)

    @block.tensor
    def _(pe):
        pe.wait_ge(loaded, 16)
        for b in range(B + 1):
            if b < B:
                if b >= 2:
                    pe.wait_ge(t_ready, b - 1)
                for t in range(QT):
                    pe.wait_ge(xn_ready, b * QT + t + 1)
                    mm = pe.transpose(psT[:, b % 2, t * P:(t + 1) * P], xn[:, b % 2, t, :], ident[:])
                mm.then_inc(t_ps, 1)
            if b:
                pe.wait_ge(t_ready, b)
                for t in range(QT):
                    mm = pe.matmul(psR[:, (b - 1) * QT + t, :], xnT[:, b - 1, t * P:(t + 1) * P], wr[:],
                                   start=True, stop=True)
        mm.then_inc(logits, 1)

    @block.scalar
    def _(act):
        for b in range(B):
            act.wait_ge(t_ps, b + 1)
            act.copy(xnT[:, b, :], psT[:, b % 2, :]).then_inc(t_ready, 1)
        act.wait_ge(logits, 1)
        act.activation(prob[:], psR[:], ACT.Sigmoid).then_inc(prob_ready, 1)


def feed_forward(nc, c, sb, ps, sem, name, a, X, xnT, comb):
    UNITS = NE * HT // 2
    C_RELU, C_SQ, C_DOWN, C_ADD, C_UP = 2, 2, 2, 3 * QT, 2
    wu = sb(c, name + "_wu", [P, NE, HID])
    wd = sb(c, name + "_wd", [P, NE, HT, D])
    relu = sb(c, name + "_relu", [P, 2, 2 * L])
    hid = sb(c, name + "_hid", [P, 2, 2, L])
    psU = ps(c, name + "_psU", [P, 2, 2, L])
    psY = ps(c, name + "_psY", [P, 3, QT, D])
    up_loaded = [sem(c, f"{name}_up_loaded{i}") for i in range(2)]
    down_loaded = [sem(c, f"{name}_down_loaded{i}") for i in range(2)]
    up = sem(c, name + "_up")
    relued = sem(c, name + "_relued")
    squared = sem(c, name + "_squared")
    down = sem(c, name + "_down")
    expert_done = sem(c, name + "_expert_done")
    added = sem(c, name + "_added")
    block = c.enter_context(nc.Block())

    @block.sync
    def _(sp):
        sp.dma_start(wu[:, 0:E, :], a["w_up"]).then_inc(up_loaded[0], 16)
        sp.dma_start(wd[:, 0:E, :, :], a["w_down"]).then_inc(down_loaded[0], 16)
        sp.dma_start(wu[:, E, :], a["w_sh_up"]).then_inc(up_loaded[1], 16)
        sp.dma_start(wd[:, E, :, :], a["w_sh_down"]).then_inc(down_loaded[1], 16)
        for i in range(2):
            sp.wait_ge(up_loaded[i], 16)
            sp.wait_ge(down_loaded[i], 16)

    @block.tensor
    def _(pe):
        pe.sem_inc(relued, C_RELU)
        pe.sem_inc(down, C_DOWN)
        pe.sem_inc(added, C_ADD)
        pe.sem_inc(squared, C_SQ)

        def up_pair(b, j, n):
            pe.wait_ge(relued, n - 2 + C_RELU + 1)
            for k in range(2):
                e, ht = j // 2, (j % 2) * 2 + k
                mm = pe.matmul(psU[:, j % 2, k, :], wu[:, e, ht * P:(ht + 1) * P],
                               xnT[:, bass.ds(b, 1), :].rearrange("p a n -> p (a n)"), start=True, stop=True)
            mm.then_inc(up, 1)

        def batch(b, last):
            for j in range(UNITS):
                n = b * UNITS + j
                if j < UNITS - 1:
                    up_pair(b, j + 1, n + 1)
                elif not last:
                    up_pair(b + 1, 0, n + 1)
                e = j // 2
                pe.wait_ge(squared, n + 1 + C_SQ)
                if j % 2 == 0:
                    pe.wait_ge(added, (b * NE + e - 2) * QT + C_ADD)
                for k in range(2):
                    ht = (j % 2) * 2 + k
                    for qt in range(QT):
                        mm = pe.matmul(psY[:, e % 3, qt, :], hid[:, j % 2, k, qt * P:(qt + 1) * P],
                                       wd[:, e, ht, :], start=(ht == 0 and qt == 0), stop=(ht == HT - 1),
                                       skip_group_check=True)
                mm.then_inc(down, 1)

        for i in range(2):
            pe.wait_ge(up_loaded[i], 16)
        up_pair(0, 0, 0)
        for i in range(2):
            pe.wait_ge(down_loaded[i], 16)
        with pe.Fori(0, B - 1) as b:
            batch(b, False)
        batch(B - 1, True)

    @block.scalar
    def _(act):
        with act.Fori(0, B) as b:
            for j in range(UNITS):
                n = b * UNITS + j
                act.wait_ge(up, n + 1)
                act.wait_ge(squared, n - 1 + C_SQ)
                act.activation(relu[:, j % 2, :], psU[:, j % 2, :, :].rearrange("p a n -> p (a n)"),
                               ACT.Relu).then_inc(relued, 1)

    @block.vector
    def _(dve):
        def add_expert(b, e):
            dve.wait_ge(down, b * UNITS + 2 * e + 2 + C_DOWN)
            for qt in range(QT):
                if e:
                    dve.wait_ge(added, (b * NE + e - 1) * QT + qt + 1 + C_ADD)
                tile = X[:, bass.ds(b * QT + qt, 1), :].rearrange("p a n -> p (a n)")
                dve.scalar_tensor_tensor(
                    out=tile, in0=psY[:, e % 3, qt, :],
                    scalar=comb[:, bass.ds(b * QT + qt, 1), e], in1=tile,
                    op0=ALU.mult, op1=ALU.add).then_inc(added, 1)

        with dve.Fori(0, B) as b:
            for j in range(UNITS):
                n = b * UNITS + j
                dve.wait_ge(relued, n + 1 + C_RELU)
                dve.wait_ge(down, n - 1 + C_DOWN)
                dve.tensor_tensor(hid[:, j % 2, :, :].rearrange("p a n -> p (a n)"), relu[:, j % 2, :],
                                  relu[:, j % 2, :], ALU.mult).then_inc(squared, 1)
                if j % 2 == 0 and j:
                    add_expert(b, j // 2 - 1)
            add_expert(b, NE - 1)


def distance_attention(nc, sb, ps, sem, a, X, V, ident, dram):
    with ExitStack() as c:
        T = sb(c, "T", [ODD + NR, 2, WIN], BF16)
        pick = sb(c, "pick", [2 * H, H, P], BF16)
        with ExitStack() as c2:
            tables(nc, c2, sb, sem, a, T, pick)
        distance_block(nc, c, sb, ps, sem, X, V, ident, dram, T, pick)


def tables(nc, c, sb, sem, a, T, pick):
    full = sb(c, "t_full", [HD, 2, WIN])
    rest = sb(c, "t_rest", [HD, 2, WIN])
    part = {w: sb(c, "t_" + w, [HD, 2, WIN], BF16) for w in "hml"}
    loaded = sem(c, "t_loaded")
    step = sem(c, "t_step")
    clear = sem(c, "t_clear")
    moved = sem(c, "t_moved")
    picked = sem(c, "t_picked")
    block = c.enter_context(nc.Block())

    @block.sync
    def _(sp):
        sp.wait_ge(clear, 2)
        sp.dma_start(full[:, 0, 0:WIN - 1], a["table_up"]).then_inc(loaded, 16)
        sp.dma_start(full[:, 1, 0:WIN - 1], a["table_down"]).then_inc(loaded, 16)
        sp.wait_ge(step, 5)
        for r, w in enumerate(RIGHT):
            sp.dma_start(T[r * HD:(r + 1) * HD, :, :], part[w][:]).then_inc(moved, 16)
            sp.dma_start(T[ODD + r * HD:ODD + (r + 1) * HD, :, 1:WIN], part[w][:, :, 0:WIN - 1]).then_inc(moved, 16)
        sp.wait_ge(moved, 32 * len(RIGHT))

    @block.vector
    def _(dve):
        dve.memset(T[:], 0.0).then_inc(clear, 1)
        dve.memset(full[:], 0.0).then_inc(clear, 1)
        dve.wait_ge(loaded, 32)
        dve.tensor_copy(part["h"][:], full[:]).then_inc(step, 1)
        dve.wait_ge(step, 1)
        dve.tensor_tensor(rest[:], full[:], part["h"][:], ALU.subtract).then_inc(step, 1)
        dve.wait_ge(step, 2)
        dve.tensor_copy(part["m"][:], rest[:]).then_inc(step, 1)
        dve.wait_ge(step, 3)
        dve.tensor_tensor(rest[:], rest[:], part["m"][:], ALU.subtract).then_inc(step, 1)
        dve.wait_ge(step, 4)
        dve.tensor_copy(part["l"][:], rest[:]).then_inc(step, 1)

    @block.gpsimd
    def _(pool):
        pool.memset(pick[:], 0.0).then_inc(picked, 1)
        for i in range(2):
            pool.wait_ge(picked, i + 1)
            pool.affine_select(out=pick[:], in_=pick[:], compare_op=ALU.not_equal, fill=1.0, base=-i * H,
                               pattern=[[-1, H], [0, P]], channel_multiplier=1).then_inc(picked, 1)


def distance_block(nc, c, sb, ps, sem, X, V, ident, dram, T, pick):
    PAIRS = P // 2
    UN = QT * QT
    HP = H // 2
    ROWS = ODD + NR
    stage = sb(c, "stage", [ROWS, 2, H, P], BF16)
    qb = sb(c, "qb", [ROWS, QT, PAIRS, 2, H], BF16)
    kb = sb(c, "kb", [ROWS, QT, PAIRS, 2, H], BF16)
    qc = sb(c, "qc", [NR, QT, H, P], BF16)
    ks = sb(c, "ks", [NR, QT, H, P], BF16)
    r1 = sb(c, "r1", [P, 2, H, P])
    r2 = sb(c, "r2", [P, 2, H, P])
    S = sb(c, "S", [P, H, L])
    W = sb(c, "W", [P, 2, 2, L])
    mx = sb(c, "mx", [P, H, QT])
    m = sb(c, "m", [P, H])
    mh = sb(c, "mh", [P, H], BF16)
    m2 = sb(c, "m2", [P, 2, H])
    mT = sb(c, "mT", [2 * H, P], BF16)
    rec = sb(c, "drec", [P, H])
    ctxt = sb(c, "ctxt", [P, H, HD])
    Vb = sb(c, "Vb", [P, GPB, QT, HG, VW])
    psR = ps(c, "psR", [P, 2, 2, L])
    psC = ps(c, "psC", [P, HP, P])
    psO = ps(c, "psDO", [P, H, VW])
    psM = ps(c, "psM", [2 * H, P])

    plan = []
    for i in range(UN + 2):
        late = i > QT and i % QT == 1
        qt = i // QT - 1
        if i < UN:
            plan += [("r1", i, 0)]
        if late:
            plan += [("m", qt, 0)]
        if i < UN:
            plan += [("r1", i, 1)]
        if late:
            for hp in range(HP):
                plan += [("e", qt, hp)] + ([("pv", qt, hp - 1)] if hp else [])
        if 0 < i <= UN:
            plan += [("c", i - 1, 0)]
        if late:
            plan += [("pv", qt, HP - 1)]
        if i < UN:
            plan += [("r2", i, 0), ("r2", i, 1)]
        if 0 < i <= UN:
            plan += [("c", i - 1, 1)]
    fills = [s for s in plan if s[0] in ("r1", "r2", "e")]
    FILLS = len(fills)
    assert FILLS % 2 == 0
    filled = {f: n + 1 for n, f in enumerate(fills)}
    UNC = 2 * UN
    C_R, C_RT, C_C, C_CT, C_PV, C_M, C_MP, C_MT, C_CTX, C_ST = FILLS, 3, UNC, 3, 3, 4, 1, 1, 3, 4

    st_loaded = [sem(c, f"st_loaded{i}") for i in range(2)]
    qc_loaded = [sem(c, f"qc_loaded{i}") for i in range(QT)]
    ks_loaded = [sem(c, f"ks_loaded{i}") for i in range(QT)]
    st_taken = sem(c, "st_taken")
    zeroed = sem(c, "zeroed")
    qb_ready = sem(c, "qb_ready")
    kb_ready = sem(c, "kb_ready")
    r_ps = sem(c, "r_ps")
    r_taken = sem(c, "r_taken")
    c_ps = sem(c, "c_ps")
    c_taken = sem(c, "c_taken")
    maxed = sem(c, "maxed")
    m_step = sem(c, "m_step")
    m_ps = sem(c, "m_ps")
    mT_ready = sem(c, "mT_ready")
    pv = sem(c, "pv")
    ctx_step = sem(c, "ctx_step")
    Vb_ready = sem(c, "Vb_ready")
    block = c.enter_context(nc.Block())
    order = [("q", 0)] + [("k", t) for t in range(QT)] + [("q", t) for t in range(1, QT)]
    NO = len(order)

    @block.sync
    def _(sp):
        with sp.Fori(0, B) as b:
            for n, (side, t) in enumerate(order):
                u = n % 2
                src = dram["qb_parts" if side == "q" else "kb_parts"]
                sp.wait_ge(st_taken, b * (2 * NO) + 2 * n - 2 + C_ST)
                for at in (0, ODD):
                    sp.dma_start(stage[at:at + NR, u, :, :], src[bass.ds(b * H, H), :, t * P:(t + 1) * P]
                                 .rearrange("h r n -> r h n")).then_inc(st_loaded[u], 16)
                if side == "q":
                    dst, src, loaded, unit = qc, "qb_parts", qc_loaded, QT * t + QT - 1
                else:
                    dst, src, loaded, unit = ks, "ks_parts", ks_loaded, UN - QT + t
                sp.wait_ge(c_ps, b * UNC + 2 * (unit + 1) - UNC + C_C)
                sp.dma_start(dst[:, t, :, :], dram[src][bass.ds(b * H, H), :, t * P:(t + 1) * P]
                             .rearrange("h r n -> r h n")).then_inc(loaded[t], 16)

    @block.gpsimd
    def _(pool):
        pool.memset(qb[:], 0.0).then_inc(zeroed, 1)
        pool.memset(kb[:], 0.0).then_inc(zeroed, 1)
        pool.wait_ge(zeroed, 2)
        with pool.Fori(0, B) as b:
            for n, (side, t) in enumerate(order):
                u = n % 2
                dst, ready = (qb, qb_ready) if side == "q" else (kb, kb_ready)
                last = ("r1", QT * t + QT - 1, 1) if side == "q" else ("r2", UN - QT + t, 1)
                pool.wait_ge(st_loaded[u], b * (16 * NO) + 32 * (n // 2 + 1))
                pool.wait_ge(r_ps, b * FILLS + filled[last] - FILLS + C_R)
                pool.sem_inc(zeroed, 1)
                for odd in range(2):
                    rows = slice(odd * ODD, odd * ODD + NR)
                    pool.tensor_copy(
                        dst[rows, t, :, odd, :],
                        stage[rows, u, :, :].rearrange("r h (n two) -> r n h two", two=2)[:, :, :, odd]
                    ).then_inc(ready, 1)
                pool.wait_ge(ready, b * (2 * QT) + 2 * t + 2)
                pool.sem_inc(st_taken, 2)

    @block.tensor
    def _(pe):
        pe.sem_inc(r_ps, C_R)
        pe.sem_inc(r_taken, C_RT)
        pe.sem_inc(c_ps, C_C)
        pe.sem_inc(c_taken, C_CT)
        pe.sem_inc(pv, C_PV)
        pe.sem_inc(m_step, C_M)
        pe.sem_inc(m_ps, C_MP)
        pe.sem_inc(mT_ready, C_MT)
        pe.sem_inc(ctx_step, C_CTX)
        pe.sem_inc(st_taken, C_ST)
        with pe.Fori(0, B) as b:
            for kind, i, part in plan:
                if (kind, i, part) in filled:
                    n = filled[kind, i, part] - 1
                    pe.wait_ge(r_taken, b * FILLS + n - 1 + C_RT)
                    slot = psR[:, n % 2, :, :]
                if kind in ("r1", "r2"):
                    qt, kt = i // QT, i % QT
                    if kind == "r1":
                        at, src, way, base = qt, qb, 1, L - 1 + P * kt - P * qt
                        pe.wait_ge(qb_ready, b * (2 * QT) + 2 * qt + 2)
                    else:
                        at, src, way, base = kt, kb, 0, L - 1 + P * qt - P * kt
                        pe.wait_ge(kb_ready, b * (2 * QT) + 2 * kt + 2)
                    for j in range(PAIRS // 2):
                        pair = part * (PAIRS // 2) + j
                        w = base - 2 * pair
                        out = slot[:, j // 16, :].rearrange("p (h n) -> p n h", h=H)
                        mm = pe.matmul(out[:, 2 * (j % 16):2 * (j % 16) + 2, :], T[:, way, w:w + P],
                                       src[:, at, pair, :, :], start=(j % 16 == 0), stop=True,
                                       skip_group_check=True)
                    mm.then_inc(r_ps, 1)
                elif kind == "m":
                    pe.wait_ge(m_step, b * (4 * QT) + 4 * (i + 1) + C_M)
                    pe.wait_ge(mT_ready, b * QT + i + C_MT)
                    pe.transpose(psM[:], m2[:].rearrange("p a h -> p (a h)"), ident[:]).then_inc(m_ps, 1)
                elif kind == "e":
                    if part == 0:
                        pe.wait_ge(mT_ready, b * QT + i + 1 + C_MT)
                    for k in range(2):
                        h = 2 * part + k
                        pe.matmul(slot[:, k, :], pick[:, h, :],
                                  mT[:].rearrange("h (a n) -> h a n", a=1).to_broadcast((2 * H, QT, P)), start=True,
                                  stop=False, skip_group_check=True)
                        for kt in range(QT):
                            mm = pe.matmul(slot[:, k, kt * P:(kt + 1) * P], S[:, h, kt * P:(kt + 1) * P],
                                           ident[:], start=False, stop=True, is_transpose=True,
                                           skip_group_check=True)
                    mm.then_inc(r_ps, 1)
                elif kind == "pv":
                    pe.wait_ge(r_taken, b * FILLS + filled["e", i, part] + C_RT)
                    if part == 0:
                        pe.wait_ge(Vb_ready, b + 1)
                        pe.wait_ge(ctx_step, b * (3 * QT) + 3 * i + C_CTX)
                    for k in range(2):
                        h = 2 * part + k
                        for kt in range(QT):
                            mm = pe.matmul(psO[:, h, :], W[:, part % 2, k, kt * P:(kt + 1) * P],
                                           Vb[:, h // HG, kt, h % HG, :],
                                           start=(h == 0 and kt == 0), stop=(kt == QT - 1),
                                           skip_group_check=True)
                    mm.then_inc(pv, 1)
                else:
                    qt, kt = i // QT, i % QT
                    pe.wait_ge(c_taken, b * UNC + 2 * i + part + C_CT)
                    if part == 0:
                        pe.wait_ge(qc_loaded[qt], b * 16 + 16)
                        pe.wait_ge(ks_loaded[kt], b * 16 + 16)
                        pe.wait_ge(r_taken, b * FILLS + filled["r1", i, 1] + C_RT)
                    for j in range(HP):
                        h = part * HP + j
                        pe.matmul(psC[:, j, :], qc[:, qt, h, :], ks[:, kt, h, :], start=(j % HG == 0),
                                  stop=False, skip_group_check=True)
                        mm = pe.matmul(psC[:, j, :], r1[:, i % 2, h, :], ident[:], start=False, stop=True,
                                       is_transpose=True, skip_group_check=True)
                    mm.then_inc(c_ps, 1)

    @block.scalar
    def _(act):
        with act.Fori(0, B) as b:
            for kind, i, part in plan:
                if kind == "m":
                    act.wait_ge(m_ps, b * QT + i + 1 + C_MP)
                    act.activation(mT[:], psM[:], ACT.Copy, scale=-1.0).then_inc(mT_ready, 1)
                if (kind, i, part) not in filled:
                    continue
                n = filled[kind, i, part] - 1
                act.wait_ge(r_ps, b * FILLS + n + 1 + C_R)
                if kind == "e":
                    act.wait_ge(pv, b * (QT * HP) + i * HP + part - 1 + C_PV)
                    act.activation(W[:, part % 2, :, :].rearrange("p a n -> p (a n)"),
                                   psR[:, n % 2, :, :].rearrange("p a n -> p (a n)"),
                                   ACT.Exp).then_inc(r_taken, 1)
                    continue
                if kind == "r1":
                    dst = r1
                    act.wait_ge(c_ps, b * UNC + 2 * (i - 1) + C_C)
                else:
                    dst = r2
                    act.wait_ge(c_taken, b * UNC + 2 * (i - 1) + C_CT)
                act.copy(dst[:, i % 2, :, part * 64:part * 64 + 64].rearrange("p h (a n) -> p a h n", a=2),
                         psR[:, n % 2, :, :].rearrange("p a (h n) -> p a h n", h=H)).then_inc(r_taken, 1)

    @block.vector
    def _(dve):
        with dve.Fori(0, B) as b:
            def context(qt):
                dve.wait_ge(pv, b * (QT * HP) + (qt + 1) * HP + C_PV)
                dve.wait_ge(ctx_step, b * (3 * QT) + 3 * qt + C_CTX)
                dve.reciprocal(rec[:], psO[:, :, HD]).then_inc(ctx_step, 1)
                dve.wait_ge(ctx_step, b * (3 * QT) + 3 * qt + 1 + C_CTX)
                dve.tensor_tensor(ctxt[:], psO[:, :, 0:HD],
                                  rec[:].rearrange("p (h a) -> p h a", a=1).to_broadcast((P, H, HD)),
                                  ALU.mult).then_inc(ctx_step, 1)
                dve.wait_ge(ctx_step, b * (3 * QT) + 3 * qt + 2 + C_CTX)
                tile = X[:, bass.ds(b * QT + qt, 1), :].rearrange("p a n -> p (a n)")
                dve.tensor_tensor(tile, tile, ctxt[:].rearrange("p h d -> p (h d)"),
                                  ALU.add).then_inc(ctx_step, 1)

            dve.wait_ge(pv, b * (QT * HP) + C_PV)
            dve.tensor_copy(Vb[:], V[:, bass.ds(b * GPB + 1, GPB), :, :, :]).then_inc(Vb_ready, 1)
            for i in range(UN):
                qt, kt = i // QT, i % QT
                for part in range(2):
                    hs = slice(part * HP, (part + 1) * HP)
                    done = 2 * i + part + 1
                    dve.wait_ge(c_ps, b * UNC + done + C_C)
                    dve.wait_ge(r_taken, b * FILLS + filled["r2", i, 1] + C_RT)
                    dve.tensor_tensor(S[:, hs, kt * P:(kt + 1) * P], psC[:], r2[:, i % 2, hs, :],
                                      ALU.add).then_inc(c_taken, 1)
                    dve.wait_ge(c_taken, b * UNC + done + C_CT)
                    dve.tensor_reduce(mx[:, hs, kt], S[:, hs, kt * P:(kt + 1) * P], AX.X,
                                      ALU.max).then_inc(maxed, 1)
                if kt == QT - 1:
                    at = b * (4 * QT) + 4 * qt + C_M
                    dve.wait_ge(maxed, b * UNC + done)
                    dve.wait_ge(m_step, at)
                    dve.tensor_reduce(m[:], mx[:], AX.X, ALU.max).then_inc(m_step, 1)
                    dve.wait_ge(m_step, at + 1)
                    dve.tensor_copy(mh[:], m[:]).then_inc(m_step, 1)
                    dve.wait_ge(m_step, at + 2)
                    dve.wait_ge(m_ps, b * QT + qt + C_MP)
                    dve.tensor_copy(m2[:, 0, :], mh[:]).then_inc(m_step, 1)
                    dve.tensor_tensor(m2[:, 1, :], m[:], mh[:], ALU.subtract).then_inc(m_step, 1)
                if kt == 0 and qt:
                    context(qt - 1)
            context(QT - 1)


INPUTS = ["L0_attn_a_x", "L0_attn_a_bq", "L0_attn_a_bk", "L0_attn_a_bv", "L0_attn_a_bo", "L0_attn_a_alpha",
          "L0_attn_a_phi", "L0_attn_a_temperature", "L0_attn_a_gamma", "L0_attn_a_beta", "L0_attn_b_bq",
          "L0_attn_b_bk", "L0_attn_b_bv", "L0_ffn_W_router"]


def kernel(**inputs):
    import concourse.bacc as _bacc
    from concourse.bass_utils import run_bass_kernel_spmd as _run

    x = {k: np.asarray(v) for k, v in inputs.items()}
    col, row = (P, 1), (1, -1)
    distance = np.arange(-(L - 1), L)
    at = MAX_POS - 1 + distance
    at = np.where(at < 0, at + 2 * MAX_POS - 1, at)
    at = np.minimum(at, 2 * MAX_POS - 2)
    table = x["L0_attn_b_dist_emb"][at].T
    data = {
        "x": x["L0_attn_a_x"],
        "temperature": x["L0_attn_a_temperature"].reshape(1, 1),
        "phi": x["L0_attn_a_phi"].reshape(row),
        "alpha": x["L0_attn_a_alpha"].reshape(row),
        "wo": x["L0_attn_a_Wo"].T,
        "bo": x["L0_attn_a_bo"].reshape(row),
        "gamma": x["L0_attn_a_gamma"].reshape(row),
        "beta": x["L0_attn_a_beta"].reshape(row),
        "w_router": x["L0_ffn_W_router"],
        "w_up": x["L0_ffn_W_up"].transpose(1, 0, 2),
        "w_sh_up": x["L0_ffn_W_sh_up"],
        "w_down": x["L0_ffn_W_down"].reshape(E, HT, P, D).transpose(2, 0, 1, 3),
        "w_sh_down": x["L0_ffn_W_sh_down"].reshape(HT, P, D).transpose(1, 0, 2),
        "table_up": table,
        "table_down": table[:, ::-1],
    }
    for layer in "ab":
        for w in "qkv":
            data[f"{layer}_w{w}"] = x[f"L0_attn_{layer}_W{w}"].T
            data[f"{layer}_b{w}"] = x[f"L0_attn_{layer}_b{w}"].reshape(row if w == "v" else col)
    data = {f"in_{k}": np.ascontiguousarray(v) for k, v in data.items()}
    nc = _bacc.Bacc("TRN2", target_bir_lowering=False, num_devices=1)
    a = {k[3:]: nc.dram_tensor(k, v.shape, mybir.dt.from_np(v.dtype), kind="ExternalInput").ap()
         for k, v in data.items()}
    a["out"] = nc.dram_tensor("out_dram", (B, L, D), F32, kind="ExternalOutput").ap()
    build(nc, a)
    r = _run(nc, [data], core_ids=[0])
    return r.results[0]["out_dram"]
```

```python
from contextlib import ExitStack

import numpy as np

import concourse.bass as bass
from concourse import mybir

F32 = mybir.dt.float32
BF16 = mybir.dt.bfloat16
I32 = mybir.dt.int32
U32 = mybir.dt.uint32
ALU = mybir.AluOpType
ACT = mybir.ActivationFunctionType
AX = mybir.AxisListType

P = 128
B, L, D = 8, 512, 128
H, HD = 16, 8
QT = L // P
NT = B * QT
HG = 4
NG = B * H // HG
GPB = H // HG
VW = HD + 1
FREQS = (31.0, 37.0, 41.0, 43.0, 47.0)
NF = len(FREQS)
PE_F = 3
TWO_PI = 2.0 * float(np.pi)
E, HID = 8, 512
NE = E + 1
HT = HID // P
MAX_POS = 256
FAR = 120.0
ACT_LAST = (0, 2, 3)
LEFT = "hhmhlm"
RIGHT = "hmhlhm"
NR = len(LEFT) * HD
ODD = 64
FRAC = 24
ROUND = float(3 * 2 ** 22)
WIN = 2 * L


def build(nc, a):
    ctx = ExitStack()
    with ctx:
        dram = {
            n: nc.dram_tensor(n, (B * H, NR, L), BF16, kind="Internal").ap()
            for n in ("qa_parts", "ka_parts", "qb_parts", "kb_parts", "ks_parts")
        }

        def sb(c, name, shape, dt=F32):
            return c.enter_context(nc.sbuf_tensor(name, shape, dt))

        def ps(c, name, shape, dt=F32):
            return c.enter_context(nc.psum_tensor(name, shape, dt))

        held = []

        def sem(c, name):
            held.append(nc.alloc_semaphore(name=name))
            return held[-1]

        def clear_semaphores():
            nc.clear_and_free_semaphores(held)
            nc.all_engine_barrier()
            held.clear()

        dram["wave_out"] = nc.dram_tensor("wave_out", (NG + 1, P, L), F32, kind="Internal").ap()
        ident = sb(ctx, "ident", [P, P])
        V = sb(ctx, "V", [P, NG + 1, QT, HG, VW])
        mv = sb(ctx, "mv", [P, NT, 2])
        rstd = sb(ctx, "rstd", [P, NT])
        with ExitStack() as c:
            params = sb(c, "params", [P, NG, 2, HG * NF])
            bound = sb(c, "bound", [P, 1])
            with ExitStack() as c2:
                X = sb(c2, "X", [P, NT, D])
                first_block(nc, sem, a, X, ident, V)
                layer_norm(nc, sb, sem, "lna", X, mv, rstd)
                project_block(nc, sb, ps, sem, "a", a, X, V, ident, mv, rstd, dram, params, bound)
            wave_attention(nc, sb, ps, sem, a, V, ident, dram, params, bound)
        X = sb(ctx, "X2", [P, NT, D])
        wave_output(nc, sb, ps, sem, a, X, ident, mv, rstd, dram)
        layer_norm(nc, sb, sem, "lnf1", X, mv, rstd)
        experts(nc, sb, ps, sem, "f1", a, X, ident, mv, rstd)
        clear_semaphores()
        layer_norm(nc, sb, sem, "lnb", X, mv, rstd)
        project_block(nc, sb, ps, sem, "b", a, X, V, ident, mv, rstd, dram, None, None)
        distance_attention(nc, sb, ps, sem, a, X, V, ident, dram)
        layer_norm(nc, sb, sem, "lnf2", X, mv, rstd)
        experts(nc, sb, ps, sem, "f2", a, X, ident, mv, rstd)
        last_block(nc, sem, a, X)


def first_block(nc, sem, a, X, ident, V):
    with ExitStack() as c:
        loaded = sem(c, "x_loaded")
        cleared = sem(c, "ident_cleared")
        made = sem(c, "ident_made")
        block = c.enter_context(nc.Block())

        @block.sync
        def _(sp):
            sp.dma_start(X[:], a["x"].rearrange("b (t p) d -> p (b t) d", p=P)).then_inc(loaded, 16)
            sp.wait_ge(loaded, 16)

        @block.gpsimd
        def _(pool):
            pool.memset(ident[:], 0.0).then_inc(cleared, 1)
            pool.wait_ge(cleared, 1)
            pool.affine_select(out=ident[:], in_=ident[:], compare_op=ALU.not_equal, fill=1.0,
                               base=0, pattern=[[-1, P]], channel_multiplier=1).then_inc(made, 1)

        @block.vector
        def _(dve):
            dve.memset(V[:], 1.0).then_inc(made, 1)


def last_block(nc, sem, a, X):
    with ExitStack() as c:
        stored = sem(c, "out_stored")
        block = c.enter_context(nc.Block())

        @block.sync
        def _(sp):
            sp.dma_start(a["out"].rearrange("b (t p) d -> p (b t) d", p=P), X[:]).then_inc(stored, 16)
            sp.wait_ge(stored, 16)


def layer_norm(nc, sb, sem, name, src, mv, rstd):
    with ExitStack() as c:
        stats = sb(c, name + "_stats", [P, NT, 6])
        var = sb(c, name + "_var", [P, NT])
        root = sb(c, name + "_root", [P, NT])
        t1 = sb(c, name + "_t1", [P, NT])
        t2 = sb(c, name + "_t2", [P, NT])
        stat = sem(c, name + "_stat")
        aggr = sem(c, name + "_aggr")
        var_ready = sem(c, name + "_var_ready")
        root_ready = sem(c, name + "_root_ready")
        step = sem(c, name + "_step")
        block = c.enter_context(nc.Block())

        @block.vector
        def _(dve):
            for t in range(NT):
                dve.bn_stats(stats[:, t, :], src[:, t, :]).then_inc(stat, 1)
            for t in range(NT):
                dve.wait_ge(stat, t + 1)
                dve.bn_aggr(mv[:, t, :], stats[:, t, :]).then_inc(aggr, 1)
            dve.wait_ge(aggr, NT)
            dve.tensor_scalar(var[:], mv[:, :, 1], 1e-5, None, ALU.add).then_inc(var_ready, 1)
            dve.wait_ge(root_ready, 1)
            dve.reciprocal(t1[:], root[:]).then_inc(step, 1)
            dve.wait_ge(step, 1)
            dve.tensor_tensor(t2[:], t1[:], t1[:], ALU.mult).then_inc(step, 1)
            dve.wait_ge(step, 2)
            dve.scalar_tensor_tensor(out=t2[:], in0=t2[:], scalar=-0.5, in1=var[:],
                                     op0=ALU.mult, op1=ALU.mult).then_inc(step, 1)
            dve.wait_ge(step, 3)
            dve.tensor_scalar(t2[:], t2[:], 1.5, None, ALU.add).then_inc(step, 1)
            dve.wait_ge(step, 4)
            dve.tensor_tensor(rstd[:], t1[:], t2[:], ALU.mult).then_inc(step, 1)

        @block.scalar
        def _(act):
            act.wait_ge(var_ready, 1)
            act.activation(root[:], var[:], ACT.Sqrt).then_inc(root_ready, 1)


def project_block(nc, sb, ps, sem, layer, a, X, V, ident, mv, rstd, dram, params, bound):
    wave = layer == "a"
    sides = [("q", "qa_parts", LEFT), ("k", "ka_parts", RIGHT)] if wave else \
            [("q", "qb_parts", LEFT), ("k", "kb_parts", LEFT), ("ks", "ks_parts", RIGHT)]
    NS = len(sides)
    with ExitStack() as c:
        wq = sb(c, layer + "_wq", [P, D])
        wk = sb(c, layer + "_wk", [P, D])
        wv = sb(c, layer + "_wv", [P, D])
        bq = sb(c, layer + "_bq", [P, 1])
        bk = sb(c, layer + "_bk", [P, 1])
        bv = sb(c, layer + "_bv", [P, D])
        qbias = sb(c, layer + "_qbias", [P, 1])
        qscale = sb(c, layer + "_qscale", [P, 1])
        xn = sb(c, layer + "_xn", [P, QT, D])
        xnT = sb(c, layer + "_xnT", [P, L])
        full = [sb(c, f"{layer}_full{s}", [P, L]) for s in range(NS)]
        rest = [sb(c, f"{layer}_rest{s}", [P, L]) for s in range(NS)]
        part = {(s, w): sb(c, f"{layer}_part{s}{w}", [P, L], BF16) for s in range(NS) for w in "hml"}
        top = sb(c, layer + "_top", [P, 2, B])
        topr = sb(c, layer + "_topr", [P, 2])
        topa = sb(c, layer + "_topa", [P, 2])
        raw = sb(c, layer + "_raw", [P, 2, H * NF])
        turns = sb(c, layer + "_turns", [P, H * NF])
        temp = sb(c, layer + "_temp", [P, 4])
        psT = ps(c, layer + "_psT", [P, L])
        psQ = ps(c, layer + "_psQ", [P, L])
        psK = ps(c, layer + "_psK", [P, L])
        psV = ps(c, layer + "_psV", [P, QT, D])
        small = sem(c, layer + "_weights_loaded")
        prep = sem(c, layer + "_prep")
        xn_ready = sem(c, layer + "_xn_ready")
        xT_ps = sem(c, layer + "_xT_ps")
        xT = sem(c, layer + "_xT")
        v_ps = sem(c, layer + "_v_ps")
        q_ps = sem(c, layer + "_q_ps")
        k_ps = sem(c, layer + "_k_ps")
        qk_taken = sem(c, layer + "_qk_taken")
        v_taken = sem(c, layer + "_v_taken")
        high = sem(c, layer + "_high")
        mid = sem(c, layer + "_mid")
        residue = sem(c, layer + "_residue")
        low = sem(c, layer + "_low")
        stored = [sem(c, f"{layer}_stored{s}") for s in range(NS)]
        topped = sem(c, layer + "_topped")
        block = c.enter_context(nc.Block())
        nload = 6 + (3 if wave else 0)

        @block.sync
        def _(sp):
            for t, src in ((wq, "wq"), (wk, "wk"), (wv, "wv")):
                sp.dma_start(t[:], a[layer + "_" + src]).then_inc(small, 16)
            for t, src in ((bq, "bq"), (bk, "bk")):
                sp.dma_start(t[:], a[layer + "_" + src]).then_inc(small, 16)
            sp.dma_start(bv[:], a[layer + "_bv"].to_broadcast((P, D))).then_inc(small, 16)
            if wave:
                sp.dma_start(temp[:, 0:1], a["temperature"].to_broadcast((P, 1))).then_inc(small, 16)
                sp.dma_start(raw[:, 0, :], a["phi"].to_broadcast((P, H * NF))).then_inc(small, 16)
                sp.dma_start(raw[:, 1, :], a["alpha"].to_broadcast((P, H * NF))).then_inc(small, 16)
            with sp.Fori(0, B) as b:
                for s, (_, dst, order) in enumerate(sides):
                    for r, w in enumerate(order):
                        if r == 0:
                            sp.wait_ge(high, b * NS + s + 1)
                        if w == "l":
                            sp.wait_ge(low, b * NS + s + 1)
                        if w == "m":
                            sp.wait_ge(mid, b * NS + s + 1)
                        sp.dma_start(
                            dram[dst][bass.ds(b * H, H), r * HD:(r + 1) * HD, :],
                            part[s, w][:]).then_inc(stored[s], 16)
            for s in range(NS):
                sp.wait_ge(stored[s], 16 * len(LEFT) * (B + 1))

        @block.vector
        def _(dve):
            dve.wait_ge(small, 16 * nload)
            if wave:
                dve.tensor_scalar(temp[:, 1:2], temp[:, 0:1], -1.0, None, ALU.mult).then_inc(prep, 1)
                dve.wait_ge(prep, 1)
                dve.tensor_tensor(temp[:, 2:3], temp[:, 0:1], temp[:, 1:2], ALU.max).then_inc(prep, 1)
                dve.wait_ge(prep, 2)
                dve.tensor_scalar(temp[:, 3:4], temp[:, 2:3], 0.1, float(np.sqrt(HD)), ALU.add,
                                  ALU.mult).then_inc(prep, 1)
                dve.wait_ge(prep, 3)
                dve.reciprocal(qscale[:], temp[:, 3:4]).then_inc(prep, 1)
                dve.wait_ge(prep, 4)
                dve.tensor_tensor(qbias[:], bq[:], qscale[:], ALU.mult).then_inc(prep, 1)
                dve.tensor_scalar(raw[:, 0, :], raw[:, 0, :], 1.0 / TWO_PI, None, ALU.mult).then_inc(prep, 1)
                dve.wait_ge(prep, 6)
                dve.tensor_scalar(turns[:], raw[:, 0, :], ROUND, ROUND, ALU.add, ALU.subtract).then_inc(prep, 1)
                dve.wait_ge(prep, 7)
                dve.tensor_tensor(raw[:, 0, :], raw[:, 0, :], turns[:], ALU.subtract).then_inc(prep, 1)
                dve.wait_ge(prep, 8)
                dve.tensor_scalar(raw[:, 0, :], raw[:, 0, :], float(2 ** FRAC), None, ALU.mult).then_inc(prep, 1)
                dve.wait_ge(prep, 9)
                for b in range(B):
                    for w in range(2):
                        dve.tensor_copy(params[:, b * GPB:(b + 1) * GPB, w, :],
                                        raw[:, w, :].rearrange("p (g n) -> p g n", g=GPB)).then_inc(prep, 1)
            else:
                dve.memset(qscale[:], 1.0).then_inc(prep, 1)
                dve.tensor_copy(qbias[:], bq[:]).then_inc(prep, 1)
            with dve.Fori(0, B) as b:
                for t in range(QT):
                    if t == 0:
                        dve.wait_ge(xT_ps, b + 1)
                    dve.tensor_scalar(xn[:, t, :], X[:, bass.ds(b * QT + t, 1), :],
                                      mv[:, bass.ds(b * QT + t, 1), 0], rstd[:, bass.ds(b * QT + t, 1)],
                                      ALU.subtract, ALU.mult).then_inc(xn_ready, 1)
                dve.wait_ge(v_ps, b + 1)
                for t in range(QT):
                    dve.tensor_tensor(
                        V[:, bass.ds(b * GPB + 1, GPB), t, :, 0:HD],
                        psV[:, t, :].rearrange("p (g h d) -> p g h d", g=GPB, h=HG),
                        bv[:].rearrange("p (g h d) -> p g h d", g=GPB, h=HG), ALU.add).then_inc(v_taken, 1)
                for s in range(NS):
                    dve.wait_ge(high, b * NS + s + 1)
                    if wave:
                        dve.tensor_reduce(top[:, s, bass.ds(b, 1)], full[s][:], AX.X, ALU.max,
                                          apply_absolute_value=True).then_inc(topped, 1)
                    dve.tensor_tensor(rest[s][:], full[s][:], part[s, "h"][:], ALU.subtract).then_inc(residue, 1)
                for s in range(NS):
                    dve.wait_ge(mid, b * NS + s + 1)
                    dve.wait_ge(stored[s], b * (16 * len(LEFT)) + 16 * len(LEFT))
                    dve.tensor_tensor(part[s, "l"][:], rest[s][:], part[s, "m"][:], ALU.subtract).then_inc(low, 1)
            if wave:
                dve.wait_ge(topped, NS * B)
                dve.tensor_reduce(topr[:], top[:], AX.X, ALU.max).then_inc(topped, 1)

        if wave:
            @block.gpsimd
            def _(pool):
                pool.wait_ge(topped, NS * B + 1)
                pool.partition_all_reduce(topa[:], topr[:], P, bass.bass_isa.ReduceOp.max).then_inc(topped, 1)
                pool.wait_ge(topped, NS * B + 2)
                pool.tensor_tensor(bound[:], topa[:, 0:1], topa[:, 1:2], ALU.mult).then_inc(topped, 1)

        @block.scalar
        def _(act):
            act.wait_ge(prep, 9 + 2 * B if wave else 2)
            with act.Fori(0, B) as b:
                act.wait_ge(xT_ps, b + 2)
                act.copy(xnT[:], psT[:]).then_inc(xT, 1)
                for s, (side, _, _) in enumerate(sides):
                    act.wait_ge(stored[s], b * (16 * len(LEFT)) + 16 * len(LEFT))
                    if side == "q":
                        act.wait_ge(q_ps, b + 1)
                        act.wait_ge(residue, b * NS + NS)
                        act.activation(full[s][:], psQ[:], ACT.Identity, bias=qbias[:], scale=qscale[:]).then_inc(qk_taken, 1)
                    elif side == "k":
                        act.wait_ge(k_ps, b + 1)
                        act.activation(full[s][:], psK[:], ACT.Identity, bias=bk[:]).then_inc(qk_taken, 1)
                    else:
                        act.wait_ge(qk_taken, b * NS + NS + 2)
                        act.mul(full[s][:], full[s - 1][:], float(1.0 / np.sqrt(HD))).then_inc(qk_taken, 1)
                    act.wait_ge(qk_taken, b * NS + s + 1 + NS)
                    act.copy(part[s, "h"][:], full[s][:]).then_inc(high, 1)
                for s in range(NS):
                    act.wait_ge(residue, b * NS + s + 1 + NS)
                    act.copy(part[s, "m"][:], rest[s][:]).then_inc(mid, 1)

        @block.tensor
        def _(pe):
            pe.sem_inc(xT_ps, 1)
            pe.sem_inc(qk_taken, NS)
            pe.sem_inc(residue, NS)
            pe.sem_inc(v_taken, QT)
            for s in range(NS):
                pe.sem_inc(stored[s], 16 * len(LEFT))
            pe.wait_ge(small, 16 * nload)
            with pe.Fori(0, B) as b:
                for t in range(QT):
                    pe.wait_ge(xn_ready, b * QT + t + 1)
                    mm = pe.transpose(psT[:, t * P:(t + 1) * P], xn[:, t, :], ident[:])
                mm.then_inc(xT_ps, 1)
                pe.wait_ge(xT, b + 1)
                pe.wait_ge(v_taken, b * QT + QT)
                for t in range(QT):
                    mm = pe.matmul(psV[:, t, :], xnT[:, t * P:(t + 1) * P], wv[:], start=True, stop=True)
                mm.then_inc(v_ps, 1)
                pe.wait_ge(qk_taken, b * NS + NS)
                pe.matmul(psQ[:], wq[:], xnT[:], start=True, stop=True).then_inc(q_ps, 1)
                pe.matmul(psK[:], wk[:], xnT[:], start=True, stop=True).then_inc(k_ps, 1)


def wave_attention(nc, sb, ps, sem, a, V, ident, dram, params, bound):
    N = QT * L
    HALF = N // 2
    SR, AR = 2, 2 * HG
    DV_F = NF - PE_F
    ADDS = 2 * DV_F
    C_SPS, C_SREADY, C_TURNED, C_LAST, C_SINE, C_USED, C_SUMMED = 2 * 2 * HG, 2, 2 * HG * (NF - 1), 2 * HG, NF, 2 * PE_F, 4
    C_ADDED, C_DIAG, C_OUT, C_TAKEN, C_STORED = 2 * HG * ADDS, 2 * HG, 2, 1, 16
    with ExitStack() as c:
        qp = sb(c, "qp", [NR, 2, HG, L], BF16)
        kp = sb(c, "kp", [NR, 2, HG, L], BF16)
        s = sb(c, "s", [P, SR, N])
        wave = sb(c, "wave", [P, 2, NF, N])
        angle = wave[:].rearrange("p a f n -> p (a f n)").bitcast(I32).rearrange(
            "p (a f n) -> p a f n", a=2, f=NF)
        score = sb(c, "score", [P, AR, N])
        par = sb(c, "par", [P, 2, 2, HG * NF])
        far = sb(c, "far", [P, 1], I32)
        diag = sb(c, "diag", [P, 2, PE_F, P])
        og = sb(c, "og", [P, L])
        Vg = sb(c, "Vg", [P, 2, QT, HG, VW])
        psS = ps(c, "psS", [P, 2, L])
        psA = ps(c, "psA", [P, QT, L])
        psO = ps(c, "psO", [P, L])
        qk_loaded = [sem(c, f"qk_loaded{i}") for i in range(2)]
        s_ps = sem(c, "s_ps")
        s_ready = sem(c, "s_ready")
        turned = sem(c, "turned")
        last_turned = sem(c, "last_turned")
        cut = sem(c, "cut")
        sine = sem(c, "sine")
        used = sem(c, "sine_used")
        par_ready = sem(c, "par_ready")
        v_ready = sem(c, "v_ready")
        diag_ready = sem(c, "diag_ready")
        summed = sem(c, "summed")
        added = sem(c, "added")
        weighed = sem(c, "weighed")
        out_ps = sem(c, "out_ps")
        out_taken = sem(c, "out_taken")
        out_stored = sem(c, "wave_stored")
        cleared = sem(c, "cleared")
        far_ready = sem(c, "far_ready")
        reduced = sem(c, "reduced")
        pool_step = sem(c, "pool_step")
        block = c.enter_context(nc.Block())

        def load(sp, g, u):
            for dst, src in ((qp, "qa_parts"), (kp, "ka_parts")):
                sp.dma_start(dst[:, u, :, :], dram[src][bass.ds(g * HG, HG), :, :]
                             .rearrange("h r n -> r h n")).then_inc(qk_loaded[u], 16)

        @block.sync
        def _(sp):
            for u in range(2):
                load(sp, u, u)

            def pair(gg, last):
                for u in range(2):
                    g = gg * 2 + u
                    sp.wait_ge(out_taken, g + 1 + C_TAKEN)
                    sp.dma_start(dram["wave_out"][bass.ds(g, 1), :, :].rearrange("g p n -> p (g n)"),
                                 og[:]).then_inc(out_stored, 16)
                    if not last:
                        sp.wait_ge(s_ps, (g + 1) * 2 * HG + C_SPS)
                        load(sp, g + 2, u)

            with sp.Fori(0, NG // 2 - 1) as gg:
                pair(gg, False)
            pair(NG // 2 - 1, True)
            sp.wait_ge(out_taken, NG + 1 + C_TAKEN)
            sp.dma_start(dram["wave_out"][NG, :, :], og[:]).then_inc(out_stored, 16)
            sp.wait_ge(out_stored, 16 * (NG + 1) + C_STORED)

        @block.gpsimd
        def _(pool):
            with pool.Fori(0, NG // 2) as gg:
                for u in range(2):
                    g = gg * 2 + u
                    pool.wait_ge(added, g * HG * ADDS + C_ADDED - HG * ADDS)
                    pool.wait_ge(turned, (g - 1) * HG * (NF - 1) + C_TURNED)
                    pool.wait_ge(last_turned, (g - 1) * HG + C_LAST)
                    pool.wait_ge(diag_ready, g * HG + C_DIAG - HG)
                    pool.tensor_copy(par[:, u, :, :], params[:, bass.ds(g, 1), :, :]
                                     .rearrange("p a w n -> p (a w) n")).then_inc(par_ready, 1)
                    pool.wait_ge(out_ps, g - 1 + C_OUT)
                    pool.sem_inc(pool_step, 1)
                    pool.tensor_copy(Vg[:, u, :, :, :], V[:, bass.ds(g, 1), :, :, :]
                                     .rearrange("p a q h d -> p (a q) h d")).then_inc(v_ready, 1)
                    pool.wait_ge(par_ready, g + 1)
                    for h in range(HG):
                        pool.wait_ge(summed, (g * HG + h) * 2 - 2 + C_SUMMED)
                        for f in range(PE_F):
                            ins = pool.tensor_tensor(diag[:, h % 2, f, :], ident[:],
                                                     par[:, u, 1, h * NF + f:h * NF + f + 1]
                                                     .to_broadcast((P, P)), ALU.mult)
                        ins.then_inc(diag_ready, 1)
            pool.wait_ge(out_ps, NG - 1 + C_OUT)
            pool.tensor_copy(Vg[:, 0, :, :, :], V[:, NG, :, :, :]).then_inc(v_ready, 1)

        @block.tensor
        def _(pe):
            for credit, n in ((s_ps, C_SPS), (s_ready, C_SREADY), (turned, C_TURNED), (last_turned, C_LAST), (sine, C_SINE),
                              (used, C_USED), (summed, C_SUMMED), (added, C_ADDED), (diag_ready, C_DIAG),
                              (out_ps, C_OUT), (out_taken, C_TAKEN),
                              (out_stored, C_STORED)):
                pe.sem_inc(credit, n)

            def make_scores(n, u, h, half):
                pe.wait_ge(s_ready, n * 2 + half + C_SREADY)
                for k in range(2):
                    kt = half * 2 + k
                    mm = pe.matmul(psS[:, k, :], kp[:, u, h, kt * P:(kt + 1) * P], qp[:, u, h, :],
                                   start=True, stop=True)
                mm.then_inc(s_ps, 1)

            def values(g, slot, heads):
                for h in heads:
                    pe.wait_ge(weighed, g * HG + h + 1)
                    if h == 0:
                        pe.wait_ge(v_ready, g + 1)
                        pe.wait_ge(out_taken, g + C_TAKEN)
                    row = h * (P // HG)
                    for kt in range(QT):
                        mm = pe.matmul(psO[row:row + VW, :],
                                       Vg[:, slot ^ 1, kt, h, :],
                                       score[:, slot * HG + h, kt * L:(kt + 1) * L],
                                       start=(kt == 0), stop=(kt == QT - 1))
                    if h == HG - 1:
                        mm.then_inc(out_ps, 1)

            def pair(gg, last):
                for u in range(2):
                    g = gg * 2 + u
                    for h in range(HG):
                        n = g * HG + h
                        more = not (last and u == 1 and h >= HG - 2)
                        nu, nh = (u, h + 2) if h < HG - 2 else (1 - u, h + 2 - HG)
                        if more:
                            if nh == 0:
                                pe.wait_ge(qk_loaded[nu], (gg + 1 + u) * 32)
                            make_scores(n + 2, nu, nh, 0)
                        pe.wait_ge(diag_ready, n + 1 + C_DIAG)
                        for f in range(PE_F):
                            pe.wait_ge(sine, n * NF + f + 1 + C_SINE)
                            for kt in range(QT):
                                if f == 0 and kt % 2 == 0:
                                    pe.wait_ge(added, n * ADDS - ADDS + kt // 2 + 1 + C_ADDED)
                                mm = pe.matmul(psA[:, kt, :], diag[:, h % 2, f, :],
                                               wave[:, h % 2, f, kt * L:(kt + 1) * L],
                                               start=(f == 0), stop=(f == PE_F - 1), skip_group_check=True)
                                if f == PE_F - 1 and kt % 2 == 1:
                                    mm.then_inc(summed, 1)
                            if f < PE_F - 1:
                                mm.then_inc(used, 1)
                            if more and f == 0:
                                make_scores(n + 2, nu, nh, 1)
                        values(g, 1 - u, {0: (0, 1), 1: (2,), 2: (3,), 3: ()}[h])

            pe.wait_ge(qk_loaded[0], 32)
            for h in range(2):
                for half in range(2):
                    make_scores(h, 0, h, half)
            with pe.Fori(0, NG // 2 - 1) as gg:
                pair(gg, False)
            pair(NG // 2 - 1, True)
            values(NG, 1, range(HG))

        @block.scalar
        def _(act):
            def take_scores(n, h, half):
                act.wait_ge(s_ps, n * 2 + half + 1 + C_SPS)
                act.wait_ge(turned, (n - 1) * (NF - 1) + C_TURNED)
                act.wait_ge(last_turned, n - 1 + C_LAST)
                act.copy(s[:, h % SR, half * HALF:(half + 1) * HALF],
                         psS[:].rearrange("p a n -> p (a n)")).then_inc(s_ready, 1)

            def last_angle(n, u, h, ng):
                f = NF - 1
                act.wait_ge(par_ready, ng + 1)
                act.wait_ge(s_ready, n * 2 + 2 + C_SREADY)
                act.wait_ge(added, n * ADDS - ADDS + C_ADDED)
                act.activation(angle[:, h % 2, f, :], s[:, h % SR, :], ACT.Identity,
                               bias=par[:, u, 0, h * NF + f:h * NF + f + 1],
                               scale=float(2 ** FRAC) / FREQS[f]).then_inc(last_turned, 1)

            def sigmoids(g, slot):
                for h in range(HG):
                    act.wait_ge(added, g * HG * ADDS - (HG - 1 - h) * ADDS + C_ADDED)
                    act.activation(score[:, slot * HG + h, :], score[:, slot * HG + h, :], ACT.Sigmoid)\
                       .then_inc(weighed, 1)

            def outputs(g):
                act.wait_ge(out_ps, g + 1 + C_OUT)
                act.wait_ge(out_stored, g * 16 + C_STORED)
                act.copy(og[:], psO[:]).then_inc(out_taken, 1)

            def pair(gg, last, general):
                for u in range(2):
                    g = gg * 2 + u
                    for h in range(HG):
                        n = g * HG + h
                        final = last and u == 1 and h == HG - 1
                        more = not (last and u == 1 and h >= HG - 2)
                        for f in range(NF):
                            act.wait_ge(cut, n * NF + f + 1)
                            act.activation(wave[:, h % 2, f, :], angle[:, h % 2, f, :], ACT.Sin,
                                           scale=float(TWO_PI / 2.0 ** 32)).then_inc(sine, 1)
                            if f in (0, 2) and more:
                                take_scores(n + 2, h + 2, f // 2)
                            if f == 2 and not final and not general and (h + 1) % HG in ACT_LAST:
                                nu, nh, ng = (u, h + 1, g) if h < HG - 1 else (1 - u, 0, g + 1)
                                last_angle(n + 1, nu, nh, ng)
                        if h == 0:
                            sigmoids(g, 1 - u)
                        if h == HG - 1:
                            outputs(g)

            def all_heads(general):
                for h in range(2):
                    for half in range(2):
                        take_scores(h, h, half)
                if not general and 0 in ACT_LAST:
                    last_angle(0, 0, 0, 0)
                act.wait_ge(cleared, 2)
                with act.Fori(0, NG // 2 - 1) as gg:
                    pair(gg, False, general)
                pair(NG // 2 - 1, True, general)
                sigmoids(NG, 1)
                outputs(NG)

            act.wait_ge(far_ready, 1)
            with act.If(act.value_load(far[0:1, 0:1])):
                all_heads(True)
            with act.Else():
                all_heads(False)

        @block.vector
        def _(dve):
            def make_turns(n, u, h, f, general):
                at = wave[:, h % 2, f, :]
                per, src, scalar = 1.0 / FREQS[f], s[:, h % SR, :], float(2 ** FRAC) / FREQS[f]
                if general:
                    k = n * (3 * NF) + 3 * f
                    dve.tensor_scalar(at, src, per, ROUND, ALU.mult, ALU.add).then_inc(reduced, 1)
                    dve.wait_ge(reduced, k + 1)
                    dve.tensor_scalar(at, at, ROUND, None, ALU.subtract).then_inc(reduced, 1)
                    dve.wait_ge(reduced, k + 2)
                    dve.scalar_tensor_tensor(out=at, in0=src, scalar=per, in1=at, op0=ALU.mult,
                                             op1=ALU.subtract).then_inc(reduced, 1)
                    dve.wait_ge(reduced, k + 3)
                    src, scalar = at, float(2 ** FRAC)
                dve.tensor_scalar(angle[:, h % 2, f, :], src, scalar, par[:, u, 0, h * NF + f:h * NF + f + 1],
                                  ALU.mult, ALU.add).then_inc(turned if f < NF - 1 else last_turned, 1)

            def make_angles(n, u, h, gs, general):
                dve.wait_ge(s_ready, gs + (h + 1) * 2 + C_SREADY)
                for f in range(NF + 1):
                    if f < NF - 1 or (f == NF - 1 and (general or h not in ACT_LAST)):
                        if f < PE_F - 1:
                            dve.wait_ge(used, (n - 2) * (PE_F - 1) + f + 1 + C_USED)
                        elif f == PE_F - 1:
                            dve.wait_ge(summed, (n - 2) * 2 + 2 + C_SUMMED)
                        else:
                            dve.wait_ge(added, n * ADDS - 2 * ADDS + 2 * (f - PE_F + 1) + C_ADDED)
                        make_turns(n, u, h, f, general)
                    if f:
                        if f < NF:
                            dve.wait_ge(turned, n * (NF - 1) + f + C_TURNED)
                        else:
                            dve.wait_ge(last_turned, n + 1 + C_LAST)
                        dve.tensor_scalar(angle[:, h % 2, f - 1, :], angle[:, h % 2, f - 1, :], 32 - FRAC, None,
                                          ALU.logical_shift_left).then_inc(cut, 1)

            def add_sine(n, u, h, f):
                dve.wait_ge(sine, n * NF + f + 1 + C_SINE)
                for half in range(2):
                    cols = slice(half * HALF, (half + 1) * HALF)
                    if f == PE_F:
                        dve.wait_ge(summed, n * 2 + half + 1 + C_SUMMED)
                        other = psA[:, half * 2:half * 2 + 2, :].rearrange("p a n -> p (a n)")
                    else:
                        dve.wait_ge(added, n * ADDS + (f - PE_F - 1) * 2 + half + 1 + C_ADDED)
                        other = score[:, u * HG + h, cols]
                    dve.scalar_tensor_tensor(
                        out=score[:, u * HG + h, cols], in0=wave[:, h % 2, f, cols],
                        scalar=par[:, u, 1, h * NF + f:h * NF + f + 1], in1=other,
                        op0=ALU.mult, op1=ALU.add).then_inc(added, 1)

            def pair(gg, last, general):
                for u in range(2):
                    g = gg * 2 + u
                    for h in range(HG):
                        n = g * HG + h
                        final = last and u == 1 and h == HG - 1
                        nu, nh, ng = (u, h + 1, g) if h < HG - 1 else (1 - u, 0, g + 1)
                        if h == HG - 1 and not final:
                            dve.wait_ge(par_ready, g + 2)
                        if not final:
                            make_angles(n + 1, nu, nh, ng * 2 * HG, general)
                        if h == 0:
                            dve.wait_ge(out_ps, g + C_OUT)
                        for f in range(PE_F, NF):
                            add_sine(n, u, h, f)

            dve.tensor_scalar(far[:], bound[:], FAR * min(FREQS) / HD, None, ALU.is_ge).then_inc(far_ready, 1)
            dve.wait_ge(far_ready, 1)
            dve.memset(score[:, HG:2 * HG, :], 0.0).then_inc(cleared, 1)
            dve.memset(psO[:], 0.0).then_inc(cleared, 1)
            dve.wait_ge(par_ready, 1)

            def all_heads(general):
                make_angles(0, 0, 0, 0, general)
                with dve.Fori(0, NG // 2 - 1) as gg:
                    pair(gg, False, general)
                pair(NG // 2 - 1, True, general)

            with dve.If(dve.value_load(far[0:1, 0:1])):
                all_heads(True)
            with dve.Else():
                all_heads(False)


def wave_output(nc, sb, ps, sem, a, X, ident, mv, rstd, dram):
    with ExitStack() as c:
        Y = sb(c, "Y", [P, NT, D])
        with ExitStack() as c2:
            wo = sb(c2, "wo", [P, D])
            bo = sb(c2, "bo", [P, D])
            o = sb(c2, "o", [P, 2, GPB, L])
            orec = sb(c2, "orec", [P, 2, QT, GPB * HG])
            oq = sb(c2, "oq", [P, QT, D])
            oT = sb(c2, "oT", [P, L])
            psG = ps(c2, "psG", [P, QT, GPB, HG, P // HG])
            psT = ps(c2, "psOT", [P, L])
            psY = ps(c2, "psY", [P, QT, D])
            loaded = sem(c2, "wo_loaded")
            o_loaded = [sem(c2, f"o_loaded{i}") for i in range(2)]
            g_ps = sem(c2, "g_ps")
            o_sum = sem(c2, "o_sum")
            o_rec = sem(c2, "o_rec")
            o_ready = sem(c2, "o_ready")
            t_ps = sem(c2, "oT_ps")
            t_ready = sem(c2, "oT_ready")
            y_ps = sem(c2, "y_ps")
            y_ready = sem(c2, "y_ready")
            block = c2.enter_context(nc.Block())

            @block.sync
            def _(sp):
                sp.sem_inc(t_ps, 1)
                sp.sem_inc(y_ready, QT)
                sp.sem_inc(o_ready, 1)
                sp.sem_inc(g_ps, 2)
                sp.dma_start(wo[:], a["wo"]).then_inc(loaded, 16)
                sp.dma_start(bo[:], a["bo"].to_broadcast((P, D))).then_inc(loaded, 16)
                sp.dma_start(X[:], a["x"].rearrange("b (t p) d -> p (b t) d", p=P)).then_inc(loaded, 16)
                with sp.Fori(0, B // 2) as bb:
                    for u in range(2):
                        sp.wait_ge(g_ps, bb * 2 + u + 1)
                        sp.dma_start(o[:, u, :, :], dram["wave_out"][bass.ds((bb * 2 + u) * GPB + 1, GPB), :, :]
                                     .rearrange("g p n -> p g n")).then_inc(o_loaded[u], 16)
                sp.wait_ge(loaded, 48)

            @block.scalar
            def _(act):
                with act.Fori(0, B) as b:
                    act.wait_ge(t_ps, b + 2)
                    act.copy(oT[:], psT[:]).then_inc(t_ready, 1)

            @block.tensor
            def _(pe):
                pe.wait_ge(loaded, 48)
                with pe.Fori(0, B // 2) as bb:
                    for u in range(2):
                        b = bb * 2 + u
                        pe.wait_ge(o_loaded[u], bb * 16 + 16)
                        pe.wait_ge(o_ready, b + 1)
                        for qt in range(QT):
                            for g in range(GPB):
                                mm = pe.transpose(psG[:, qt, g, :, :].rearrange("p h n -> p (h n)"),
                                                  o[:, u, g, qt * P:(qt + 1) * P], ident[:])
                        mm.then_inc(g_ps, 1)
                        pe.wait_ge(o_ready, b + 2)
                        for qt in range(QT):
                            mm = pe.transpose(psT[:, qt * P:(qt + 1) * P], oq[:, qt, :], ident[:])
                        mm.then_inc(t_ps, 1)
                        pe.wait_ge(t_ready, b + 1)
                        pe.wait_ge(y_ready, b * QT + QT)
                        for qt in range(QT):
                            mm = pe.matmul(psY[:, qt, :], oT[:, qt * P:(qt + 1) * P], wo[:], start=True, stop=True)
                        mm.then_inc(y_ps, 1)

            @block.vector
            def _(dve):
                dve.wait_ge(loaded, 48)
                with dve.Fori(0, B) as b:
                    dve.wait_ge(g_ps, b + 3)
                    dve.tensor_scalar(orec[:, 0, :, :], psG[:, :, :, :, HD].rearrange("p q g h -> p q (g h)"),
                                      1e-10, None, ALU.add).then_inc(o_sum, 1)
                    dve.wait_ge(o_sum, b + 1)
                    dve.reciprocal(orec[:, 1, :, :], orec[:, 0, :, :]).then_inc(o_rec, 1)
                    dve.wait_ge(o_rec, b + 1)
                    dve.wait_ge(t_ps, b + 1)
                    dve.tensor_tensor(oq[:].rearrange("p q (h d) -> p q h d", h=H),
                                      psG[:, :, :, :, 0:HD].rearrange("p q g h d -> p q (g h) d"),
                                      orec[:, 1, :, :].rearrange("p q (h o) -> p q h o", o=1)
                                      .to_broadcast((P, QT, H, HD)), ALU.mult).then_inc(o_ready, 1)
                    dve.wait_ge(y_ps, b + 1)
                    for qt in range(QT):
                        dve.tensor_tensor(Y[:, bass.ds(b * QT + qt, 1), :].rearrange("p a n -> p (a n)"),
                                          psY[:, qt, :], bo[:], ALU.add).then_inc(y_ready, 1)
        layer_norm(nc, sb, sem, "lny", Y, mv, rstd)
        with ExitStack() as c2:
            gamma = sb(c2, "gamma", [P, D])
            beta = sb(c2, "beta", [P, D])
            loaded = sem(c2, "gamma_loaded")
            step = sem(c2, "apply")
            block = c2.enter_context(nc.Block())
            HALF_T = NT // 2

            @block.sync
            def _(sp):
                sp.dma_start(gamma[:], a["gamma"].to_broadcast((P, D))).then_inc(loaded, 16)
                sp.dma_start(beta[:], a["beta"].to_broadcast((P, D))).then_inc(loaded, 16)
                sp.wait_ge(loaded, 32)

            @block.vector
            def _(dve):
                for t in range(NT):
                    dve.tensor_scalar(Y[:, t, :], Y[:, t, :], mv[:, t, 0:1], rstd[:, t:t + 1],
                                      ALU.subtract, ALU.mult).then_inc(step, 1)
                dve.wait_ge(loaded, 32)
                dve.wait_ge(step, NT)
                wide = (P, NT, D)
                dve.tensor_tensor(Y[:], Y[:], gamma[:].rearrange("p (o d) -> p o d", o=1).to_broadcast(wide),
                                  ALU.mult).then_inc(step, 1)
                dve.tensor_tensor(X[:], X[:], beta[:].rearrange("p (o d) -> p o d", o=1).to_broadcast(wide),
                                  ALU.add).then_inc(step, 1)
                dve.wait_ge(step, NT + 2)
                dve.tensor_tensor(X[:], X[:], Y[:], ALU.add).then_inc(step, 1)


def experts(nc, sb, ps, sem, name, a, X, ident, mv, rstd):
    with ExitStack() as c:
        xnT = sb(c, name + "_xnT", [P, B, L])
        comb = sb(c, name + "_comb", [P, NT, NE])
        with ExitStack() as c2:
            route(nc, c2, sb, ps, sem, name, a, X, ident, mv, rstd, xnT, comb)
        with ExitStack() as c2:
            feed_forward(nc, c2, sb, ps, sem, name, a, X, xnT, comb)


def route(nc, c, sb, ps, sem, name, a, X, ident, mv, rstd, xnT, comb):
    wr = sb(c, name + "_wr", [P, E])
    xn = sb(c, name + "_xn", [P, 2, QT, D])
    prob = sb(c, name + "_prob", [P, NT, E])
    top = sb(c, name + "_top", [P, NT, E])
    index = sb(c, name + "_index", [P, NT, E], U32)
    indexf = sb(c, name + "_indexf", [P, NT, 2])
    iota = sb(c, name + "_iota", [P, E])
    first = sb(c, name + "_first", [P, NT, E])
    total = sb(c, name + "_total", [P, NT])
    psT = ps(c, name + "_psT", [P, 2, L])
    psR = ps(c, name + "_psR", [P, NT, E])
    loaded = sem(c, name + "_wr_loaded")
    xn_ready = sem(c, name + "_xn_ready")
    t_ps = sem(c, name + "_t_ps")
    t_ready = sem(c, name + "_t_ready")
    logits = sem(c, name + "_logits")
    prob_ready = sem(c, name + "_prob_ready")
    iota_ready = sem(c, name + "_iota_ready")
    step = sem(c, name + "_route_step")
    block = c.enter_context(nc.Block())

    @block.sync
    def _(sp):
        sp.dma_start(wr[:], a["w_router"]).then_inc(loaded, 16)
        sp.wait_ge(loaded, 16)

    @block.gpsimd
    def _(pool):
        pool.iota(iota[:], pattern=[[1, E]], base=0, channel_multiplier=0,
                  allow_small_or_imprecise_dtypes=True).then_inc(iota_ready, 1)

    @block.vector
    def _(dve):
        for t in range(NT):
            if t >= 2 * QT and t % QT == 0:
                dve.wait_ge(t_ps, t // QT - 1)
            dve.tensor_scalar(xn[:, (t // QT) % 2, t % QT, :], X[:, t, :], mv[:, t, 0:1], rstd[:, t:t + 1],
                              ALU.subtract, ALU.mult).then_inc(xn_ready, 1)
        dve.wait_ge(prob_ready, 1)
        for t in range(NT):
            dve.max(top[:, t, :], prob[:, t, :]).then_inc(step, 1)
        for t in range(NT):
            dve.wait_ge(step, t + 1)
            dve.max_index(index[:, t, :], top[:, t, :], prob[:, t, :]).then_inc(step, 1)
        dve.wait_ge(step, 2 * NT)
        dve.tensor_copy(indexf[:], index[:, :, 0:2]).then_inc(step, 1)
        dve.tensor_tensor(total[:], top[:, :, 0], top[:, :, 1], ALU.add).then_inc(step, 1)
        dve.wait_ge(step, 2 * NT + 2)
        dve.tensor_scalar(total[:], total[:], 1e-6, None, ALU.add).then_inc(step, 1)
        dve.wait_ge(step, 2 * NT + 3)
        dve.reciprocal(total[:], total[:]).then_inc(step, 1)
        dve.wait_ge(iota_ready, 1)
        wide = (P, NT, E)
        places = iota[:].rearrange("p (o e) -> p o e", o=1).to_broadcast(wide)
        dve.wait_ge(step, 2 * NT + 4)
        dve.tensor_tensor(first[:], places, indexf[:, :, 0:1].to_broadcast(wide), ALU.is_equal).then_inc(step, 1)
        dve.tensor_tensor(comb[:, :, 0:E], places, indexf[:, :, 1:2].to_broadcast(wide), ALU.is_equal)\
           .then_inc(step, 1)
        dve.memset(comb[:, :, E:NE], 1.0).then_inc(step, 1)
        dve.wait_ge(step, 2 * NT + 6)
        dve.tensor_tensor(first[:], first[:], top[:, :, 0:1].to_broadcast(wide), ALU.mult).then_inc(step, 1)
        dve.tensor_tensor(comb[:, :, 0:E], comb[:, :, 0:E], top[:, :, 1:2].to_broadcast(wide), ALU.mult)\
           .then_inc(step, 1)
        dve.wait_ge(step, 2 * NT + 9)
        dve.tensor_tensor(comb[:, :, 0:E], comb[:, :, 0:E], first[:], ALU.add).then_inc(step, 1)
        dve.wait_ge(step, 2 * NT + 10)
        dve.tensor_tensor(comb[:, :, 0:E], comb[:, :, 0:E],
                          total[:].rearrange("p (t o) -> p t o", o=1).to_broadcast(wide), ALU.mult)\
           .then_inc(step, 1)

    @block.tensor
    def _(pe):
        pe.wait_ge(loaded, 16)
        for b in range(B + 1):
            if b < B:
                if b >= 2:
                    pe.wait_ge(t_ready, b - 1)
                for t in range(QT):
                    pe.wait_ge(xn_ready, b * QT + t + 1)
                    mm = pe.transpose(psT[:, b % 2, t * P:(t + 1) * P], xn[:, b % 2, t, :], ident[:])
                mm.then_inc(t_ps, 1)
            if b:
                pe.wait_ge(t_ready, b)
                for t in range(QT):
                    mm = pe.matmul(psR[:, (b - 1) * QT + t, :], xnT[:, b - 1, t * P:(t + 1) * P], wr[:],
                                   start=True, stop=True)
        mm.then_inc(logits, 1)

    @block.scalar
    def _(act):
        for b in range(B):
            act.wait_ge(t_ps, b + 1)
            act.copy(xnT[:, b, :], psT[:, b % 2, :]).then_inc(t_ready, 1)
        act.wait_ge(logits, 1)
        act.activation(prob[:], psR[:], ACT.Sigmoid).then_inc(prob_ready, 1)


def feed_forward(nc, c, sb, ps, sem, name, a, X, xnT, comb):
    UNITS = NE * HT // 2
    C_RELU, C_SQ, C_DOWN, C_ADD, C_UP = 2, 2, 2, 3 * QT, 2
    wu = sb(c, name + "_wu", [P, NE, HID])
    wd = sb(c, name + "_wd", [P, NE, HT, D])
    relu = sb(c, name + "_relu", [P, 2, 2 * L])
    hid = sb(c, name + "_hid", [P, 2, 2, L])
    psU = ps(c, name + "_psU", [P, 2, 2, L])
    psY = ps(c, name + "_psY", [P, 3, QT, D])
    up_loaded = [sem(c, f"{name}_up_loaded{i}") for i in range(2)]
    down_loaded = [sem(c, f"{name}_down_loaded{i}") for i in range(2)]
    up = sem(c, name + "_up")
    relued = sem(c, name + "_relued")
    squared = sem(c, name + "_squared")
    down = sem(c, name + "_down")
    expert_done = sem(c, name + "_expert_done")
    added = sem(c, name + "_added")
    block = c.enter_context(nc.Block())

    @block.sync
    def _(sp):
        sp.dma_start(wu[:, 0:E, :], a["w_up"]).then_inc(up_loaded[0], 16)
        sp.dma_start(wd[:, 0:E, :, :], a["w_down"]).then_inc(down_loaded[0], 16)
        sp.dma_start(wu[:, E, :], a["w_sh_up"]).then_inc(up_loaded[1], 16)
        sp.dma_start(wd[:, E, :, :], a["w_sh_down"]).then_inc(down_loaded[1], 16)
        for i in range(2):
            sp.wait_ge(up_loaded[i], 16)
            sp.wait_ge(down_loaded[i], 16)

    @block.tensor
    def _(pe):
        pe.sem_inc(relued, C_RELU)
        pe.sem_inc(down, C_DOWN)
        pe.sem_inc(added, C_ADD)
        pe.sem_inc(squared, C_SQ)

        def up_pair(b, j, n):
            pe.wait_ge(relued, n - 2 + C_RELU + 1)
            for k in range(2):
                e, ht = j // 2, (j % 2) * 2 + k
                mm = pe.matmul(psU[:, j % 2, k, :], wu[:, e, ht * P:(ht + 1) * P],
                               xnT[:, bass.ds(b, 1), :].rearrange("p a n -> p (a n)"), start=True, stop=True)
            mm.then_inc(up, 1)

        def batch(b, last):
            for j in range(UNITS):
                n = b * UNITS + j
                if j < UNITS - 1:
                    up_pair(b, j + 1, n + 1)
                elif not last:
                    up_pair(b + 1, 0, n + 1)
                e = j // 2
                pe.wait_ge(squared, n + 1 + C_SQ)
                if j % 2 == 0:
                    pe.wait_ge(added, (b * NE + e - 2) * QT + C_ADD)
                for k in range(2):
                    ht = (j % 2) * 2 + k
                    for qt in range(QT):
                        mm = pe.matmul(psY[:, e % 3, qt, :], hid[:, j % 2, k, qt * P:(qt + 1) * P],
                                       wd[:, e, ht, :], start=(ht == 0 and qt == 0), stop=(ht == HT - 1),
                                       skip_group_check=True)
                mm.then_inc(down, 1)

        for i in range(2):
            pe.wait_ge(up_loaded[i], 16)
        up_pair(0, 0, 0)
        for i in range(2):
            pe.wait_ge(down_loaded[i], 16)
        with pe.Fori(0, B - 1) as b:
            batch(b, False)
        batch(B - 1, True)

    @block.scalar
    def _(act):
        with act.Fori(0, B) as b:
            for j in range(UNITS):
                n = b * UNITS + j
                act.wait_ge(up, n + 1)
                act.wait_ge(squared, n - 1 + C_SQ)
                act.activation(relu[:, j % 2, :], psU[:, j % 2, :, :].rearrange("p a n -> p (a n)"),
                               ACT.Relu).then_inc(relued, 1)

    @block.vector
    def _(dve):
        def add_expert(b, e):
            dve.wait_ge(down, b * UNITS + 2 * e + 2 + C_DOWN)
            for qt in range(QT):
                if e:
                    dve.wait_ge(added, (b * NE + e - 1) * QT + qt + 1 + C_ADD)
                tile = X[:, bass.ds(b * QT + qt, 1), :].rearrange("p a n -> p (a n)")
                dve.scalar_tensor_tensor(
                    out=tile, in0=psY[:, e % 3, qt, :],
                    scalar=comb[:, bass.ds(b * QT + qt, 1), e], in1=tile,
                    op0=ALU.mult, op1=ALU.add).then_inc(added, 1)

        with dve.Fori(0, B) as b:
            for j in range(UNITS):
                n = b * UNITS + j
                dve.wait_ge(relued, n + 1 + C_RELU)
                dve.wait_ge(down, n - 1 + C_DOWN)
                dve.tensor_tensor(hid[:, j % 2, :, :].rearrange("p a n -> p (a n)"), relu[:, j % 2, :],
                                  relu[:, j % 2, :], ALU.mult).then_inc(squared, 1)
                if j % 2 == 0 and j:
                    add_expert(b, j // 2 - 1)
            add_expert(b, NE - 1)


def distance_attention(nc, sb, ps, sem, a, X, V, ident, dram):
    with ExitStack() as c:
        T = sb(c, "T", [ODD + NR, 2, WIN], BF16)
        pick = sb(c, "pick", [2 * H, H, P], BF16)
        with ExitStack() as c2:
            tables(nc, c2, sb, sem, a, T, pick)
        distance_block(nc, c, sb, ps, sem, X, V, ident, dram, T, pick)


def tables(nc, c, sb, sem, a, T, pick):
    full = sb(c, "t_full", [HD, 2, WIN])
    rest = sb(c, "t_rest", [HD, 2, WIN])
    part = {w: sb(c, "t_" + w, [HD, 2, WIN], BF16) for w in "hml"}
    loaded = sem(c, "t_loaded")
    step = sem(c, "t_step")
    clear = sem(c, "t_clear")
    moved = sem(c, "t_moved")
    picked = sem(c, "t_picked")
    block = c.enter_context(nc.Block())

    @block.sync
    def _(sp):
        sp.wait_ge(clear, 2)
        sp.dma_start(full[:, 0, 0:WIN - 1], a["table_up"]).then_inc(loaded, 16)
        sp.dma_start(full[:, 1, 0:WIN - 1], a["table_down"]).then_inc(loaded, 16)
        sp.wait_ge(step, 5)
        for r, w in enumerate(RIGHT):
            sp.dma_start(T[r * HD:(r + 1) * HD, :, :], part[w][:]).then_inc(moved, 16)
            sp.dma_start(T[ODD + r * HD:ODD + (r + 1) * HD, :, 1:WIN], part[w][:, :, 0:WIN - 1]).then_inc(moved, 16)
        sp.wait_ge(moved, 32 * len(RIGHT))

    @block.vector
    def _(dve):
        dve.memset(T[:], 0.0).then_inc(clear, 1)
        dve.memset(full[:], 0.0).then_inc(clear, 1)
        dve.wait_ge(loaded, 32)
        dve.tensor_copy(part["h"][:], full[:]).then_inc(step, 1)
        dve.wait_ge(step, 1)
        dve.tensor_tensor(rest[:], full[:], part["h"][:], ALU.subtract).then_inc(step, 1)
        dve.wait_ge(step, 2)
        dve.tensor_copy(part["m"][:], rest[:]).then_inc(step, 1)
        dve.wait_ge(step, 3)
        dve.tensor_tensor(rest[:], rest[:], part["m"][:], ALU.subtract).then_inc(step, 1)
        dve.wait_ge(step, 4)
        dve.tensor_copy(part["l"][:], rest[:]).then_inc(step, 1)

    @block.gpsimd
    def _(pool):
        pool.memset(pick[:], 0.0).then_inc(picked, 1)
        for i in range(2):
            pool.wait_ge(picked, i + 1)
            pool.affine_select(out=pick[:], in_=pick[:], compare_op=ALU.not_equal, fill=1.0, base=-i * H,
                               pattern=[[-1, H], [0, P]], channel_multiplier=1).then_inc(picked, 1)


def distance_block(nc, c, sb, ps, sem, X, V, ident, dram, T, pick):
    PAIRS = P // 2
    UN = QT * QT
    HP = H // 2
    ROWS = ODD + NR
    stage = sb(c, "stage", [ROWS, 2, H, P], BF16)
    qb = sb(c, "qb", [ROWS, QT, PAIRS, 2, H], BF16)
    kb = sb(c, "kb", [ROWS, QT, PAIRS, 2, H], BF16)
    qc = sb(c, "qc", [NR, QT, H, P], BF16)
    ks = sb(c, "ks", [NR, QT, H, P], BF16)
    r1 = sb(c, "r1", [P, 2, H, P])
    r2 = sb(c, "r2", [P, 2, H, P])
    S = sb(c, "S", [P, H, L])
    W = sb(c, "W", [P, 2, 2, L])
    mx = sb(c, "mx", [P, H, QT])
    m = sb(c, "m", [P, H])
    mh = sb(c, "mh", [P, H], BF16)
    m2 = sb(c, "m2", [P, 2, H])
    mT = sb(c, "mT", [2 * H, P], BF16)
    rec = sb(c, "drec", [P, H])
    ctxt = sb(c, "ctxt", [P, H, HD])
    oS = sb(c, "oS", [P, L])
    Vb = sb(c, "Vb", [P, GPB, QT, HG, VW])
    psR = ps(c, "psR", [P, 2, 2, L])
    psC = ps(c, "psC", [P, HP, P])
    psO = ps(c, "psDO", [P, GPB, P])
    psG = ps(c, "psDG", [P, GPB, HG, P // HG])

    def steps(first, last, more):
        out = []
        for i in range(first, last):
            late = i > QT and i % QT == 1
            qt = i // QT - 1
            fill = i < UN or more
            unit, nb = (i, 0) if i < UN else (i - UN, 1)
            prev, pb = (i - 1, 0) if i <= UN else (i - 1 - UN, 1)
            content = 0 < i <= UN or (i > UN and more)
            if fill:
                out += [("r1", unit, 0, nb)]
            if fill:
                out += [("r1", unit, 1, nb)]
            if late:
                out += [("m", qt, 0, 0)]
                for hp in range(HP):
                    out += [("e", qt, hp, 0)] + ([("pv", qt, hp - 1, 0)] if hp else [])
            if content:
                out += [("c", prev, 0, pb)]
            if late:
                out += [("pv", qt, HP - 1, 0)]
            if fill:
                out += [("r2", unit, 0, nb)]
            if late:
                out += [("o", qt, 0, 0)]
            if fill:
                out += [("r2", unit, 1, nb)]
            if content:
                out += [("c", prev, 1, pb)]
        return out

    def fills(plan):
        return {s: n + 1 for n, s in enumerate(s for s in plan if s[0] in ("r1", "r2", "m", "e"))}

    FIRST, BODY, LAST = steps(0, 2, False), steps(2, UN + 2, True), steps(2, UN + 2, False)
    filled = fills(BODY)
    PRO, FILLS = len(fills(FIRST)), len(filled)
    assert PRO % 2 == 0 and FILLS % 2 == 0
    UNC = 2 * UN

    def all_batches(eng, run):
        def go(plan, b, base):
            here = fills(plan)
            run(plan, b, base, lambda *step: base + here.get(step, 0))

        go(FIRST, 0, 0)
        with eng.Fori(0, B - 1) as b:
            go(BODY, b, PRO + b * FILLS)
        go(LAST, B - 1, PRO + (B - 1) * FILLS)

    C_R, C_RT, C_C, C_CT, C_PV, C_M, C_MT, C_CTX, C_ST, C_O, C_G = PRO + FILLS, 3, UNC, 3, 3, 4, 1, 3, 4, 1, 1

    st_loaded = [sem(c, f"st_loaded{i}") for i in range(2)]
    qc_loaded = [sem(c, f"qc_loaded{i}") for i in range(QT)]
    ks_loaded = [sem(c, f"ks_loaded{i}") for i in range(QT)]
    st_taken = sem(c, "st_taken")
    zeroed = sem(c, "zeroed")
    qb_ready = sem(c, "qb_ready")
    kb_ready = sem(c, "kb_ready")
    r_ps = sem(c, "r_ps")
    r_taken = sem(c, "r_taken")
    c_ps = sem(c, "c_ps")
    c_taken = sem(c, "c_taken")
    maxed = sem(c, "maxed")
    m_step = sem(c, "m_step")
    o_taken = sem(c, "o_taken")
    g_ps = sem(c, "dg_ps")
    psO_clear = sem(c, "psO_clear")
    mT_ready = sem(c, "mT_ready")
    pv = sem(c, "pv")
    ctx_step = sem(c, "ctx_step")
    Vb_ready = sem(c, "Vb_ready")
    block = c.enter_context(nc.Block())
    order = [("q", 0)] + [("k", t) for t in range(QT)] + [("q", t) for t in range(1, QT)]
    NO = len(order)

    @block.sync
    def _(sp):
        with sp.Fori(0, B) as b:
            for n, (side, t) in enumerate(order):
                u = n % 2
                src = dram["qb_parts" if side == "q" else "kb_parts"]
                sp.wait_ge(st_taken, b * (2 * NO) + 2 * n - 2 + C_ST)
                for at in (0, ODD):
                    sp.dma_start(stage[at:at + NR, u, :, :], src[bass.ds(b * H, H), :, t * P:(t + 1) * P]
                                 .rearrange("h r n -> r h n")).then_inc(st_loaded[u], 16)
                if side == "q":
                    dst, src, loaded, unit = qc, "qb_parts", qc_loaded, QT * t + QT - 1
                else:
                    dst, src, loaded, unit = ks, "ks_parts", ks_loaded, UN - QT + t
                sp.wait_ge(c_ps, b * UNC + 2 * (unit + 1) - UNC + C_C)
                sp.dma_start(dst[:, t, :, :], dram[src][bass.ds(b * H, H), :, t * P:(t + 1) * P]
                             .rearrange("h r n -> r h n")).then_inc(loaded[t], 16)

    @block.gpsimd
    def _(pool):
        pool.memset(qb[:], 0.0).then_inc(zeroed, 1)
        pool.memset(kb[:], 0.0).then_inc(zeroed, 1)
        pool.wait_ge(zeroed, 2)
        with pool.Fori(0, B) as b:
            for n, (side, t) in enumerate(order):
                u = n % 2
                dst, ready = (qb, qb_ready) if side == "q" else (kb, kb_ready)
                last = ("r1", QT * t + QT - 1, 1, 0) if side == "q" else ("r2", UN - QT + t, 1, 0)
                pool.wait_ge(st_loaded[u], b * (16 * NO) + 32 * (n // 2 + 1))
                pool.wait_ge(r_ps, b * FILLS + PRO + filled[last] - FILLS + C_R)
                pool.sem_inc(zeroed, 1)
                for odd in range(2):
                    rows = slice(odd * ODD, odd * ODD + NR)
                    pool.tensor_copy(
                        dst[rows, t, :, odd, :],
                        stage[rows, u, :, :].rearrange("r h (n two) -> r n h two", two=2)[:, :, :, odd]
                    ).then_inc(ready, 1)
                pool.wait_ge(ready, b * (2 * QT) + 2 * t + 2)
                pool.sem_inc(st_taken, 2)

    @block.tensor
    def _(pe):
        pe.sem_inc(r_ps, C_R)
        pe.sem_inc(r_taken, C_RT)
        pe.sem_inc(c_ps, C_C)
        pe.sem_inc(c_taken, C_CT)
        pe.sem_inc(pv, C_PV)
        pe.sem_inc(m_step, C_M)
        pe.sem_inc(o_taken, C_O)
        pe.sem_inc(g_ps, C_G)
        pe.sem_inc(mT_ready, C_MT)
        pe.sem_inc(ctx_step, C_CTX)
        pe.sem_inc(st_taken, C_ST)

        def run(plan, batch, base, count):
            here = fills(plan)
            for step in plan:
                kind, i, part, nb = step
                b = batch + nb
                if step in here:
                    n = here[step] - 1
                    pe.wait_ge(r_taken, base + n - 1 + C_RT)
                    slot = psR[:, n % 2, :, :]
                if kind in ("r1", "r2"):
                    qt, kt = i // QT, i % QT
                    if kind == "r1":
                        at, src, way, w0 = qt, qb, 1, L - 1 + P * kt - P * qt
                        pe.wait_ge(qb_ready, b * (2 * QT) + 2 * qt + 2)
                    else:
                        at, src, way, w0 = kt, kb, 0, L - 1 + P * qt - P * kt
                        pe.wait_ge(kb_ready, b * (2 * QT) + 2 * kt + 2)
                    for j in range(PAIRS // 2):
                        pair = part * (PAIRS // 2) + j
                        w = w0 - 2 * pair
                        out = slot[:, j // 16, :].rearrange("p (h n) -> p n h", h=H)
                        mm = pe.matmul(out[:, 2 * (j % 16):2 * (j % 16) + 2, :], T[:, way, w:w + P],
                                       src[:, at, pair, :, :], start=(j % 16 == 0), stop=True,
                                       skip_group_check=True)
                    mm.then_inc(r_ps, 1)
                elif kind == "m":
                    pe.wait_ge(m_step, b * (4 * QT) + 4 * (i + 1) + C_M)
                    pe.transpose(slot[0:2 * H, 0, 0:P], m2[:].rearrange("p a h -> p (a h)"),
                                 ident[:]).then_inc(r_ps, 1)
                elif kind == "e":
                    if part == 0:
                        pe.wait_ge(mT_ready, b * QT + i + 1 + C_MT)
                    for k in range(2):
                        h = 2 * part + k
                        pe.matmul(slot[:, k, :], pick[:, h, :],
                                  mT[:].rearrange("h (a n) -> h a n", a=1).to_broadcast((2 * H, QT, P)), start=True,
                                  stop=False, skip_group_check=True)
                        for kt in range(QT):
                            mm = pe.matmul(slot[:, k, kt * P:(kt + 1) * P], S[:, h, kt * P:(kt + 1) * P],
                                           ident[:], start=False, stop=True, is_transpose=True,
                                           skip_group_check=True)
                    mm.then_inc(r_ps, 1)
                elif kind == "pv":
                    pe.wait_ge(r_taken, count("e", i, part, 0) + C_RT)
                    if part == 0:
                        pe.wait_ge(Vb_ready, b + 1)
                        pe.wait_ge(o_taken, b * QT + i + C_O)
                    for k in range(2):
                        h = 2 * part + k
                        for kt in range(QT):
                            row = (h % HG) * (P // HG)
                            mm = pe.matmul(psO[row:row + VW, h // HG, :], Vb[:, h // HG, kt, h % HG, :],
                                           W[:, part % 2, k, kt * P:(kt + 1) * P],
                                           start=(kt == 0), stop=(kt == QT - 1),
                                           skip_group_check=True)
                    mm.then_inc(pv, 1)
                elif kind == "o":
                    pe.wait_ge(o_taken, b * QT + i + 1 + C_O)
                    pe.wait_ge(ctx_step, b * (3 * QT) + 3 * i + C_CTX)
                    for g in range(GPB):
                        mm = pe.transpose(psG[:, g, :, :].rearrange("p h n -> p (h n)"),
                                          oS[:, g * P:(g + 1) * P], ident[:])
                    mm.then_inc(g_ps, 1)
                else:
                    qt, kt = i // QT, i % QT
                    pe.wait_ge(c_taken, b * UNC + 2 * i + part + C_CT)
                    if part == 0:
                        pe.wait_ge(qc_loaded[qt], b * 16 + 16)
                        pe.wait_ge(ks_loaded[kt], b * 16 + 16)
                        pe.wait_ge(r_taken, count("r1", i, 1, nb) + C_RT)
                    for j in range(HP):
                        h = part * HP + j
                        pe.matmul(psC[:, j, :], qc[:, qt, h, :], ks[:, kt, h, :], start=(j % HG == 0),
                                  stop=False, skip_group_check=True)
                        mm = pe.matmul(psC[:, j, :], r1[:, i % 2, h, :], ident[:], start=False, stop=True,
                                       is_transpose=True, skip_group_check=True)
                    mm.then_inc(c_ps, 1)

        all_batches(pe, run)

    @block.scalar
    def _(act):
        def run(plan, batch, base, count):
            here = fills(plan)
            for step in plan:
                kind, i, part, nb = step
                b = batch + nb
                if kind == "pv" and part == HP - 1:
                    act.wait_ge(pv, b * (QT * HP) + (i + 1) * HP + C_PV)
                    act.wait_ge(g_ps, b * QT + i + C_G)
                    act.copy(oS[:], psO[:].rearrange("p g n -> p (g n)")).then_inc(o_taken, 1)
                if step not in here:
                    continue
                n = here[step] - 1
                act.wait_ge(r_ps, base + n + 1 + C_R)
                if kind == "m":
                    act.activation(mT[:], psR[0:2 * H, n % 2, 0, 0:P], ACT.Copy, scale=-1.0).then_inc(mT_ready, 1)
                    act.wait_ge(mT_ready, b * QT + i + 1 + C_MT)
                    act.sem_inc(r_taken, 1)
                    continue
                if kind == "e":
                    act.wait_ge(pv, b * (QT * HP) + i * HP + part - 1 + C_PV)
                    act.activation(W[:, part % 2, :, :].rearrange("p a n -> p (a n)"),
                                   psR[:, n % 2, :, :].rearrange("p a n -> p (a n)"),
                                   ACT.Exp).then_inc(r_taken, 1)
                    continue
                if kind == "r1":
                    dst = r1
                    act.wait_ge(c_ps, b * UNC + 2 * (i - 1) + C_C)
                else:
                    dst = r2
                    act.wait_ge(c_taken, b * UNC + 2 * (i - 1) + C_CT)
                act.copy(dst[:, i % 2, :, part * 64:part * 64 + 64].rearrange("p h (a n) -> p a h n", a=2),
                         psR[:, n % 2, :, :].rearrange("p a (h n) -> p a h n", h=H)).then_inc(r_taken, 1)

        all_batches(act, run)

    @block.vector
    def _(dve):
        dve.memset(psO[:], 0.0).then_inc(psO_clear, 1)
        dve.wait_ge(psO_clear, 1)
        def values(b):
            dve.wait_ge(pv, b * (QT * HP) + C_PV)
            dve.tensor_copy(Vb[:], V[:, bass.ds(b * GPB + 1, GPB), :, :, :]).then_inc(Vb_ready, 1)

        def context(b, qt):
            at = b * (3 * QT) + 3 * qt + C_CTX
            dve.wait_ge(g_ps, b * QT + qt + 1 + C_G)
            dve.wait_ge(ctx_step, at)
            dve.reciprocal(rec[:], psG[:, :, :, HD].rearrange("p g h -> p (g h)")).then_inc(ctx_step, 1)
            dve.wait_ge(ctx_step, at + 1)
            dve.tensor_tensor(ctxt[:], psG[:, :, :, 0:HD].rearrange("p g h d -> p (g h) d"),
                              rec[:].rearrange("p (h a) -> p h a", a=1).to_broadcast((P, H, HD)),
                              ALU.mult).then_inc(ctx_step, 1)
            dve.wait_ge(ctx_step, at + 2)
            tile = X[:, bass.ds(b * QT + qt, 1), :].rearrange("p a n -> p (a n)")
            dve.tensor_tensor(tile, tile, ctxt[:].rearrange("p h d -> p (h d)"),
                              ALU.add).then_inc(ctx_step, 1)

        def maximum(b, qt, count):
            at = b * (4 * QT) + 4 * qt + C_M
            dve.wait_ge(maxed, b * UNC + 2 * QT * (qt + 1))
            dve.wait_ge(m_step, at)
            dve.tensor_reduce(m[:], mx[:], AX.X, ALU.max).then_inc(m_step, 1)
            dve.wait_ge(m_step, at + 1)
            dve.tensor_copy(mh[:], m[:]).then_inc(m_step, 1)
            dve.wait_ge(m_step, at + 2)
            dve.wait_ge(r_ps, count("m", qt - 1, 0, 0) + C_R)
            dve.tensor_copy(m2[:, 0, :], mh[:]).then_inc(m_step, 1)
            dve.tensor_tensor(m2[:, 1, :], m[:], mh[:], ALU.subtract).then_inc(m_step, 1)

        def run(plan, batch, base, count):
            for kind, i, part, nb in plan:
                b = batch + nb
                if kind == "o":
                    context(b, i)
                    if i == QT - 1 and plan is BODY:
                        values(b + 1)
                if kind != "c":
                    continue
                kt = i % QT
                hs = slice(part * HP, (part + 1) * HP)
                done = b * UNC + 2 * i + part + 1
                dve.wait_ge(c_ps, done + C_C)
                dve.wait_ge(r_taken, count("r2", i, 1, nb) + C_RT)
                dve.tensor_tensor(S[:, hs, kt * P:(kt + 1) * P], psC[:], r2[:, i % 2, hs, :],
                                  ALU.add).then_inc(c_taken, 1)
                dve.wait_ge(c_taken, done + C_CT)
                dve.tensor_reduce(mx[:, hs, kt], S[:, hs, kt * P:(kt + 1) * P], AX.X,
                                  ALU.max).then_inc(maxed, 1)
                if kt == QT - 1 and part == 1:
                    maximum(b, i // QT, count)

        values(0)
        all_batches(dve, run)


INPUTS = ["L0_attn_a_x", "L0_attn_a_bq", "L0_attn_a_bk", "L0_attn_a_bv", "L0_attn_a_bo", "L0_attn_a_alpha",
          "L0_attn_a_phi", "L0_attn_a_temperature", "L0_attn_a_gamma", "L0_attn_a_beta", "L0_attn_b_bq",
          "L0_attn_b_bk", "L0_attn_b_bv", "L0_ffn_W_router"]


def kernel(**inputs):
    import concourse.bacc as _bacc
    from concourse.bass_utils import run_bass_kernel_spmd as _run

    x = {k: np.asarray(v) for k, v in inputs.items()}
    col, row = (P, 1), (1, -1)
    distance = np.arange(-(L - 1), L)
    at = MAX_POS - 1 + distance
    at = np.where(at < 0, at + 2 * MAX_POS - 1, at)
    at = np.minimum(at, 2 * MAX_POS - 2)
    table = x["L0_attn_b_dist_emb"][at].T
    data = {
        "x": x["L0_attn_a_x"],
        "temperature": x["L0_attn_a_temperature"].reshape(1, 1),
        "phi": x["L0_attn_a_phi"].reshape(row),
        "alpha": x["L0_attn_a_alpha"].reshape(row),
        "wo": x["L0_attn_a_Wo"].T,
        "bo": x["L0_attn_a_bo"].reshape(row),
        "gamma": x["L0_attn_a_gamma"].reshape(row),
        "beta": x["L0_attn_a_beta"].reshape(row),
        "w_router": x["L0_ffn_W_router"],
        "w_up": x["L0_ffn_W_up"].transpose(1, 0, 2),
        "w_sh_up": x["L0_ffn_W_sh_up"],
        "w_down": x["L0_ffn_W_down"].reshape(E, HT, P, D).transpose(2, 0, 1, 3),
        "w_sh_down": x["L0_ffn_W_sh_down"].reshape(HT, P, D).transpose(1, 0, 2),
        "table_up": table,
        "table_down": table[:, ::-1],
    }
    for layer in "ab":
        for w in "qkv":
            data[f"{layer}_w{w}"] = x[f"L0_attn_{layer}_W{w}"].T
            data[f"{layer}_b{w}"] = x[f"L0_attn_{layer}_b{w}"].reshape(row if w == "v" else col)
    data = {f"in_{k}": np.ascontiguousarray(v) for k, v in data.items()}
    nc = _bacc.Bacc("TRN2", target_bir_lowering=False, num_devices=1)
    a = {k[3:]: nc.dram_tensor(k, v.shape, mybir.dt.from_np(v.dtype), kind="ExternalInput").ap()
         for k, v in data.items()}
    a["out"] = nc.dram_tensor("out_dram", (B, L, D), F32, kind="ExternalOutput").ap()
    build(nc, a)
    r = _run(nc, [data], core_ids=[0])
    return r.results[0]["out_dram"]
```
